# Optimizing a Trainium2 kernel written in Bass

```python
import numpy as np
import jax
import jax.numpy as jnp

def _softmax(x, axis=-1):
    return jax.nn.softmax(x, axis=axis)

def _gelu(x):
    return jax.nn.gelu(x, approximate=True)

def _silu(x):
    return jax.nn.silu(x)

def _sigmoid(x):
    return jax.nn.sigmoid(x)

def _layernorm(x, axis=-1, eps=1e-05):
    m = jnp.mean(x, axis=axis, keepdims=True)
    v = jnp.var(x, axis=axis, keepdims=True)
    return (x - m) / jnp.sqrt(v + eps)

def _scatter_add(tgt, idx, src, axis=0):
    return tgt.at[idx].add(src)

def _segment_sum(src, seg, n):
    return jax.ops.segment_sum(src, seg, n)
kernel_name = 'mk_decoder_postln_d1_seqx_r8_23e088'

def setup_inputs(seed: int=0):
    np.random.seed(seed)
    _w = jnp.asarray

    def _rec_inputs():
        import jax
        import jax.numpy as jnp
        _rk = jax.random.key(seed)
        x = -0.000125 + 0.9999 * jax.random.normal(jax.random.fold_in(_rk, 1), (4, 256, 256), jnp.float32)
        _lenS = 256 - jax.random.randint(jax.random.fold_in(_rk, 7), (4,), 0, max(1, 256 // 4) + 1, jnp.int32)
        _lenS2 = 256 - jax.random.randint(jax.random.fold_in(_rk, 8), (4,), 0, max(1, 256 // 4) + 1, jnp.int32)
        itok_BxS_13_99985 = jax.random.randint(jax.random.fold_in(_rk, 11), (4, 256), 13, 99986, jnp.int32)
        _ctx_2048P = jax.random.normal(jax.random.fold_in(_rk, 12), (4, 16, 256), jnp.float32)
        _ctx_2048c = jax.random.dirichlet(jax.random.fold_in(_rk, 512), 0.3 * jnp.ones((16,), jnp.float32), (4, 256))
        _ctx_2048t = jnp.einsum('bsk,bkd->bsd', _ctx_2048c, _ctx_2048P)
        _ctx_2048t = _ctx_2048t * jax.lax.rsqrt(jnp.mean(jnp.square(_ctx_2048t)) + 1e-12) * 0.953939
        ctx_2048 = 6.82029e-06 + 0.0200006 * (_ctx_2048t + 0.3 * jax.random.normal(jax.random.fold_in(_rk, 612), (4, 256, 256), jnp.float32))
        return (x, itok_BxS_13_99985, ctx_2048)
    x, itok_BxS_13_99985, ctx_2048 = _rec_inputs()

    def _L0_attn_setup():
        import jax, jax.numpy as jnp
        import numpy as np
        IN_FEATURES = 256
        HEAD_NUM = 64
        D = IN_FEATURES // HEAD_NUM
        SCALE = float(np.sqrt(D))
        key = jax.random.key(seed)
        ks = jax.random.split(key, 9)
        F = IN_FEATURES
        x = jax.random.normal(ks[0], (4, 128, F), dtype=jnp.float32)
        w = lambda k: jax.random.normal(k, (F, F), dtype=jnp.float32) * 0.02
        b = lambda k: jax.random.normal(k, (F,), dtype=jnp.float32) * 0.01
        return {'x': x, 'Wq': w(ks[1]), 'bq': b(ks[2]), 'Wk': w(ks[3]), 'bk': b(ks[4]), 'Wv': w(ks[5]), 'bv': b(ks[6]), 'Wo': w(ks[7]), 'bo': b(ks[8])}
    _L0_attn_all = _L0_attn_setup()
    _L0_attn_in = {k: v for k, v in _L0_attn_all.items() if k in ('Wq', 'bq', 'Wk', 'bk', 'Wv', 'bv', 'Wo', 'bo')}
    del _L0_attn_all

    def _L0_xattn_setup():
        import jax, jax.numpy as jnp
        import numpy as np
        B, S, D = (4, 512, 256)
        E = 4
        F = 1024 // E
        VOCAB = 12500
        key = jax.random.key(seed)
        k1, k2, k3, k4, k5 = jax.random.split(key, 5)
        hidden_states = jax.random.normal(k1, (B, S, D), dtype=jnp.float32)
        token_ids = jax.random.randint(k2, (B, S), 0, VOCAB, dtype=jnp.int64)
        Wg = jax.random.normal(k3, (E, F, D), dtype=jnp.float32) * 0.02
        Wu = jax.random.normal(k4, (E, F, D), dtype=jnp.float32) * 0.02
        Wd = jax.random.normal(k5, (E, D, F), dtype=jnp.float32) * 0.02
        return {'hidden_states': hidden_states, 'token_ids': token_ids, 'Wg': Wg, 'Wu': Wu, 'Wd': Wd}
    _L0_xattn_all = _L0_xattn_setup()
    _L0_xattn_in = {k: v for k, v in _L0_xattn_all.items() if k in ()}
    del _L0_xattn_all

    def _L0_ffn_setup():
        import jax, jax.numpy as jnp
        import numpy as np
        TURBO_BLOCK_SIZE = 64
        TURBO_MSE_BITS = 5
        QMAX = 2 ** (TURBO_MSE_BITS - 1) - 1
        SHRINKS = np.linspace(0.4, 1.0, 16)

        def mse_quant_dequant(w):
            O, I = w.shape
            wb = w.reshape(O, I // TURBO_BLOCK_SIZE, TURBO_BLOCK_SIZE)
            amax = jnp.max(jnp.abs(wb), axis=-1, keepdims=True)
            base = jnp.maximum(amax, 1e-08) / QMAX
            best_err = jnp.full(amax.shape, jnp.inf, dtype=w.dtype)
            best_scale = base
            for s in SHRINKS:
                scale = base * jnp.asarray(s, dtype=w.dtype)
                deq = jnp.clip(jnp.round(wb / scale), -QMAX, QMAX) * scale
                err = jnp.sum((deq - wb) ** 2, axis=-1, keepdims=True)
                upd = err < best_err
                best_err = jnp.where(upd, err, best_err)
                best_scale = jnp.where(upd, scale, best_scale)
            deq = jnp.clip(jnp.round(wb / best_scale), -QMAX, QMAX) * best_scale
            return deq.reshape(O, I)

        def turbo_linear(x, w):
            wq = w + jax.lax.stop_gradient(mse_quant_dequant(w) - w)
            return x @ wq.T
        key = jax.random.key(seed)
        k1, k2, k3 = jax.random.split(key, 3)
        dim, mlp_mult = (256, 4)
        hidden = mlp_mult * dim
        x = jax.random.normal(k1, (4, 256, dim), dtype=jnp.float32)
        w_fc = jax.random.normal(k2, (hidden, dim), dtype=jnp.float32) * 0.02
        w_proj = jax.random.normal(k3, (dim, hidden), dtype=jnp.float32) * 0.02
        return {'x': x, 'w_fc': w_fc, 'w_proj': w_proj}
    _L0_ffn_all = _L0_ffn_setup()
    _L0_ffn_in = {k: v for k, v in _L0_ffn_all.items() if k in ('w_fc', 'w_proj')}
    del _L0_ffn_all
    return {'x': x, 'itok_BxS_13_99985': itok_BxS_13_99985, 'ctx_2048': ctx_2048, 'L0_attn_Wq': _L0_attn_in['Wq'], 'L0_attn_bq': _L0_attn_in['bq'], 'L0_attn_Wk': _L0_attn_in['Wk'], 'L0_attn_bk': _L0_attn_in['bk'], 'L0_attn_Wv': _L0_attn_in['Wv'], 'L0_attn_bv': _L0_attn_in['bv'], 'L0_attn_Wo': _L0_attn_in['Wo'], 'L0_attn_bo': _L0_attn_in['bo'], 'L0_ffn_w_fc': _L0_ffn_in['w_fc'], 'L0_ffn_w_proj': _L0_ffn_in['w_proj']}

def reference(x, itok_BxS_13_99985, ctx_2048, L0_attn_Wq, L0_attn_bq, L0_attn_Wk, L0_attn_bk, L0_attn_Wv, L0_attn_bv, L0_attn_Wo, L0_attn_bo, L0_ffn_w_fc, L0_ffn_w_proj):
    import jax
    import jax.numpy as jnp

    def _L0_attn_ref(x, Wq, bq, Wk, bk, Wv, bv, Wo, bo):
        import jax, jax.numpy as jnp
        import numpy as np
        IN_FEATURES = 256
        HEAD_NUM = 64
        D = IN_FEATURES // HEAD_NUM
        SCALE = float(np.sqrt(D))
        B, S, F = x.shape
        d = D
        h = F // d
        q = x @ Wq + bq
        k = x @ Wk + bk
        v = x @ Wv + bv

        def to_heads(t):
            return t.reshape(B, S, d, h).transpose(0, 2, 1, 3)
        q, k, v = (to_heads(q), to_heads(k), to_heads(v))
        scores = jnp.einsum('bdsh,bdth->bdst', q, k) / SCALE
        weights = jax.nn.softmax(scores, axis=-1)
        feats = jnp.einsum('bdst,bdth->bdsh', weights, v)
        feats = feats.transpose(0, 2, 1, 3).reshape(B, S, F)
        return feats @ Wo + bo

    def _L0_xattn_ref(hidden_states, token_ids, Wg, Wu, Wd):
        import jax, jax.numpy as jnp
        import numpy as np
        B, S, D = (4, 512, 256)
        E = 4
        F = 1024 // E
        VOCAB = 12500
        tokens_per_expert = VOCAB // E
        tid = jnp.clip(token_ids, 0, VOCAB - 1)
        expert_ids = jnp.minimum(tid // tokens_per_expert, E - 1)
        out = jnp.zeros_like(hidden_states)
        for e in range(E):
            g = jax.nn.silu(jnp.einsum('bsd,fd->bsf', hidden_states, Wg[e]))
            u = jnp.einsum('bsd,fd->bsf', hidden_states, Wu[e])
            y = jnp.einsum('bsf,df->bsd', g * u, Wd[e])
            out = jnp.where((expert_ids == e)[..., None], y, out)
        return out

    def _L0_ffn_ref(x, w_fc, w_proj):
        import jax, jax.numpy as jnp
        import numpy as np
        TURBO_BLOCK_SIZE = 64
        TURBO_MSE_BITS = 5
        QMAX = 2 ** (TURBO_MSE_BITS - 1) - 1
        SHRINKS = np.linspace(0.4, 1.0, 16)

        def mse_quant_dequant(w):
            O, I = w.shape
            wb = w.reshape(O, I // TURBO_BLOCK_SIZE, TURBO_BLOCK_SIZE)
            amax = jnp.max(jnp.abs(wb), axis=-1, keepdims=True)
            base = jnp.maximum(amax, 1e-08) / QMAX
            best_err = jnp.full(amax.shape, jnp.inf, dtype=w.dtype)
            best_scale = base
            for s in SHRINKS:
                scale = base * jnp.asarray(s, dtype=w.dtype)
                deq = jnp.clip(jnp.round(wb / scale), -QMAX, QMAX) * scale
                err = jnp.sum((deq - wb) ** 2, axis=-1, keepdims=True)
                upd = err < best_err
                best_err = jnp.where(upd, err, best_err)
                best_scale = jnp.where(upd, scale, best_scale)
            deq = jnp.clip(jnp.round(wb / best_scale), -QMAX, QMAX) * best_scale
            return deq.reshape(O, I)

        def turbo_linear(x, w):
            wq = w + jax.lax.stop_gradient(mse_quant_dequant(w) - w)
            return x @ wq.T
        h = jnp.maximum(turbo_linear(x, w_fc), 0.0)
        return turbo_linear(h * h, w_proj)
    x = _layernorm(x + _L0_attn_ref(x, L0_attn_Wq, L0_attn_bq, L0_attn_Wk, L0_attn_bk, L0_attn_Wv, L0_attn_bv, L0_attn_Wo, L0_attn_bo), axis=-1)
    x = _layernorm(x + _L0_xattn_ref(x, itok_BxS_13_99985, ctx_2048, ctx_2048, ctx_2048), axis=-1)
    x = _layernorm(x + _L0_ffn_ref(x, L0_ffn_w_fc, L0_ffn_w_proj), axis=-1)
    return x

_drawn_inputs = setup_inputs


def setup_inputs(seed=0):
    import zlib

    import numpy as np

    out = dict(_drawn_inputs(seed))
    spreads = {}
    factors = {'L0_attn_Wq': 8.0,
     'L0_attn_bq': 8.0,
     'L0_attn_Wk': 8.0,
     'L0_attn_bk': 64.0,
     'L0_attn_Wv': 8.0,
     'L0_attn_bv': 8.0,
     'L0_attn_Wo': 7.877,
     'L0_attn_bo': 36.142}
    for name, (base, spread) in spreads.items():
        noise = np.random.default_rng([zlib.crc32(name.encode()), seed]).standard_normal(out[name].shape)
        drawn = base * np.exp(spread * noise) if base else spread * noise
        out[name] = jnp.asarray(drawn.astype(out[name].dtype))
    for name, factor in factors.items():
        out[name] = (out[name] * factor).astype(out[name].dtype)
    return out
```

```python
from contextlib import ExitStack

import numpy as np
import concourse.bass as bass
from concourse import mybir

F32 = mybir.dt.float32
I32 = mybir.dt.int32
U8 = mybir.dt.uint8
BF16 = mybir.dt.bfloat16
ALU = mybir.AluOpType
ACT = mybir.ActivationFunctionType
AX = mybir.AxisListType

P = 128
B, T, F = 4, 256, 256
HEADS, DH = 4, 64
E = 4
HID = 1024
ST = T // P
KT = F // P
OT = HID // P
VOCAB = 12500
PER_EXPERT = VOCAB // E
EPS = 1e-5
QBLK = 64
QMAX = 15
SHRINKS = [float(np.float32(s)) for s in np.linspace(0.4, 1.0, 16)]
NS = len(SHRINKS)
CH = 1024
NCH = 2 * HID * F // (P * CH)
NB = CH // QBLK
RING = 3
ROUND = 1.5 * 2.0 ** 23
FAR = 1000.0

assert NCH == B


def build_decoder(nc, x, tok, ctx_w, Wq, bq, Wk, bk, Wv, bv, Wo, bo, w_fc, w_proj, out):
    with ExitStack() as ctx:
        def sb(name, shape, dt=F32):
            return ctx.enter_context(nc.sbuf_tensor(name, shape, dt))

        def bank(name):
            return ctx.enter_context(nc.psum_tensor(name, [P, 512], F32))

        def sem(name):
            return ctx.enter_context(nc.semaphore(name))

        wq_s, wk_s, wv_s, wo_s = (sb(n, [P, KT, F]) for n in ("wq_s", "wk_s", "wv_s", "wo_s"))
        bq_s, bk_s, bv_s = (sb(n, [P, KT]) for n in ("bq_s", "bk_s", "bv_s"))
        bqh = sb("bqh", [P, KT])
        bo_bc = sb("bo_bc", [P, F])
        cxT = sb("cxT", [P, E, KT, F])
        tok_bc = sb("tok_bc", [P, B * T], I32)
        mask = sb("mask", [P, E, B * T], BF16)
        below = sb("below", [P, 2, B * T], BF16)
        ident = sb("ident", [P, P])
        shrink = sb("shrink", [P, NS])
        eps_s = sb("eps_s", [P, ST])
        mhalf = sb("mhalf", [P, ST])
        w_nat = sb("w_nat", [P, NCH, CH])
        wT = sb("wT", [P, NCH, CH // P, P])

        x_nat = sb("x_nat", [P, ST, F])
        xb = sb("xb", [P, ST, F])
        xT = sb("xT", [P, KT, T])
        qT = sb("qT", [P, KT, T])
        kTs = sb("kTs", [P, KT, T])
        v_s = sb("v_s", [P, ST, F])
        nmax = sb("nmax", [P, HEADS, ST])
        rsum = sb("rsum", [P, HEADS, ST])
        rinv = sb("rinv", [P, HEADS, ST])
        prob = sb("prob", [P, HEADS, ST, T])
        probT = sb("probT", [P, HEADS, ST, T])
        feat = sb("feat", [P, ST, F])
        featT = sb("featT", [P, KT, T])
        r1 = sb("r1", [P, ST, F])
        x1 = sb("x1", [P, ST, F])
        x1T = sb("x1T", [P, E, KT, T])
        tanh_s = sb("tanh_s", [P, KT, T])
        u_s = sb("u_s", [P, KT, T])
        p_s = sb("p_s", [P, KT, T])
        pm = sb("pm", [P, E, KT, T])
        r2 = sb("r2", [P, ST, F])
        x2 = sb("x2", [P, ST, F])
        x2_all = sb("x2_all", [P, B, ST, F])
        x2T = sb("x2T", [P, KT, B * T])
        bst = sb("bst", [P, ST, 6])
        mv = sb("mv", [P, ST, 2])
        veps = sb("veps", [P, ST])
        rstd = sb("rstd", [P, ST])
        base = sb("base", [P, NB])
        amax = sb("amax", [P, NB])
        rbase = sb("rbase", [P, NB])
        a_n = sb("a_n", [P, CH])
        z_s = sb("z_s", [P, RING, CH], U8)
        g_s = sb("g_s", [P, RING, CH])
        cx_nat = g_s[:, 0:2, :].rearrange("p a (e k f) -> p (a e) k f", k=KT, f=F)
        e_s = sb("e_s", [P, RING, CH])
        errs = sb("errs", [P, NS, NB])
        emin = sb("emin", [P, NB])
        cand = sb("cand", [P, NS, NB])
        best = sb("best", [P, NB])
        scale = sb("scale", [P, NB])
        rscale = sb("rscale", [P, NB])
        t_w = sb("t_w", [P, CH])
        deq = t_w
        wq_nat = sb("wq_nat", [P, CH])
        relu_s = sb("relu_s", [P, 2, 2, T])
        h2T = prob[:, :, :, :].rearrange("p h s t -> p (h s) t")
        r3 = sb("r3", [P, ST, F])
        y_out = sb("y_out", [P, ST, F])

        tr_ps = bank("tr_ps")
        pt_ps = bank("pt_ps")
        s_ps = [bank("s0_ps"), bank("s1_ps")]
        a_ps, b_ps, c_ps, w_ps = bank("a_ps"), bank("b_ps"), bank("c_ps"), bank("w_ps")

        def two(ps):
            return ps[:, :].rearrange("p (a t) -> p a t", a=2)

        per = dict(
            x_loaded=16, x_cast=1, xT_ready=1, xT_sb=1, xb_ready=1,
            q_ready=1, q_sb=2, k_ready=1, k_sb=2, v_ready=1, v_sb=1,
            s_ready=HEADS, nmax_ready=HEADS, p_sb=HEADS * ST, pt_ready=HEADS, pt_sb=HEADS,
            f_ready=1, rinv_ready=1, f_sb=1, fT_ready=1, fT_sb=KT, o_ready=1, r1_ready=1,
            bst1=ST, mv1=ST, ve1=1, rstd1=1, x1_ready=ST, x1T_ready=1, x1T_sb=E,
            h_ready=1, tanh_ready=1, u_ready=1, p_ready=1, pm_ready=E, y_ready=1, r2_ready=1,
            bst2=ST, mv2=ST, ve2=1, rstd2=1, x2_ready=ST, x2T_ready=1, x2T_sb=1, x2_kept=16,
            amax_ready=1, base_ready=1, rbase_ready=1, ratio_ready=1, a_ready=1,
            z_ready=NS, g_ready=NS, e_ready=NS, err_ready=NS,
            emin_ready=1, ne_ready=1, cand_ready=1, best_ready=1, scale_ready=1, rscale_ready=1,
            tw_ready=1, tc_ready=1, qw_ready=1, deq_ready=1, ddq_ready=1, wq_ready=1,
            wT_ready=2, wT_sb=2,
            f1_ready=OT // 2, relu_ready=OT // 2, h2_ready=OT // 2, f2_ready=1, r3_ready=1,
            bst3=ST, mv3=ST, ve3=1, rstd3=1, y_sb=ST, y_kept=16,
        )
        S = {name: sem(name) for name in per}
        once = {name: sem(name) for name in (
            "wqk_loaded", "wvo_loaded", "b_loaded", "bo_loaded", "cx_loaded", "tok_loaded", "w_loaded",
            "zero_ready", "ident_ready", "const_ready", "bqh_ready", "shrink_ready", "below_ready", "mask_ready", "cxT_ready", "cxT_sb")}

        primed = ("f2_ready", "p_ready", "r1_ready", "r2_ready", "r3_ready", "relu_ready", "wT_ready", "wT_sb", "wq_ready", "x2T_sb", "x2_kept", "y_kept")

        def wait(eng, name, b, n):
            eng.wait_ge(S[name], b * per[name] + n + (name in primed))

        dve_tick = sb("dve_tick", [P, 3])
        pool_tick = sb("pool_tick", [P, NS])

        block = ctx.enter_context(nc.Block())

        @block.sync
        def _(sp):
            def load_x(b):
                sp.dma_start(x_nat[:, :, :].rearrange("p (a s) f -> p a s f", a=1),
                             x[bass.ds(b, 1), :, :].rearrange("a (s p) f -> p a s f", p=P)
                             ).then_inc(S["x_loaded"], 16)

            def rows(w):
                return w.rearrange("(k p) n -> p k n", p=P)

            for name in primed:
                sp.sem_inc(S[name], 1)
            load_x(0)
            sp.dma_start(wq_s[:, :, :], rows(Wq)).then_inc(once["wqk_loaded"], 16)
            sp.dma_start(wk_s[:, :, :], rows(Wk)).then_inc(once["wqk_loaded"], 16)
            for s, d in ((bq_s, bq), (bk_s, bk), (bv_s, bv)):
                sp.dma_start(s[:, :], d.rearrange("(k p) -> p k", p=P), allow_slow_non_contiguous=True).then_inc(once["b_loaded"], 16)
            for c in range(NCH // 2):
                sp.dma_start(w_nat[:, c, :].rearrange("p (o i) -> p o i", i=F),
                             w_fc[c * CH * P // F:(c + 1) * CH * P // F, :].rearrange("(o p) i -> p o i", p=P)
                             ).then_inc(once["w_loaded"], 16)
            sp.dma_start(wv_s[:, :, :], rows(Wv)).then_inc(once["wvo_loaded"], 16)
            sp.dma_start(wo_s[:, :, :], rows(Wo)).then_inc(once["wvo_loaded"], 16)
            sp.dma_start(bo_bc[:, :], bo.rearrange("(a f) -> a f", a=1).broadcast_to([P, F])
                         ).then_inc(once["bo_loaded"], 16)
            sp.dma_start(tok_bc[:, :], tok.rearrange("b t -> (b t)").rearrange("(a n) -> a n", a=1)
                         .broadcast_to([P, B * T])).then_inc(once["tok_loaded"], 16)
            sp.dma_start(cx_nat[:, :, :, :], ctx_w.rearrange("e (k p) d -> p e k d", p=P)
                         ).then_inc(once["cx_loaded"], 16)
            for c in range(NCH // 2):
                sp.dma_start(w_nat[:, NCH // 2 + c, :], w_proj[c * P:(c + 1) * P, :]
                             ).then_inc(once["w_loaded"], 16)
            with sp.Fori(0, B - 1) as b:
                wait(sp, "xT_ready", b, 1)
                wait(sp, "xb_ready", b, 1)
                load_x(b + 1)
                wait(sp, "x2_ready", b, ST)
                sp.dma_start(x2_all[:, bass.ds(b, 1), :, :],
                             x2[:, :, :].rearrange("p (a s) f -> p a s f", a=1)).then_inc(S["x2_kept"], 16)
            wait(sp, "x2_ready", B - 1, ST)
            sp.dma_start(x2_all[:, B - 1, :, :], x2[:, :, :]).then_inc(S["x2_kept"], 16)
            with sp.Fori(0, B) as b:
                wait(sp, "y_sb", b, ST)
                sp.dma_start(out[bass.ds(b, 1), :, :].rearrange("a (s p) f -> p a s f", p=P),
                             y_out[:, :, :].rearrange("p (a s) f -> p a s f", a=1)).then_inc(S["y_kept"], 16)
            wait(sp, "y_kept", B - 1, 16)

        @block.gpsimd
        def _(pool):
            pool.memset(ident[:, :], 0.0).then_inc(once["zero_ready"], 1)
            pool.wait_ge(once["zero_ready"], 1)
            pool.affine_select(out=ident[:, :], in_=ident[:, :], compare_op=ALU.not_equal, fill=1.0,
                               base=0, pattern=[[-1, P]], channel_multiplier=1).then_inc(once["ident_ready"], 1)
            pool.memset(mhalf[:, :], -0.5).then_inc(once["const_ready"], 1)
            pool.memset(eps_s[:, :], EPS).then_inc(once["const_ready"], 1)
            pool.wait_ge(once["const_ready"], 2)
            pool.wait_ge(once["bo_loaded"], 16)

            def inv_std(b, mv_name, ve_name, rstd_name):
                wait(pool, mv_name, b, ST)
                pool.tensor_tensor(veps[:, :], mv[:, :, 1], eps_s[:, :], ALU.add).then_inc(S[ve_name], 1)
                wait(pool, ve_name, b, 1)
                pool.tensor_tensor(rstd[:, :], veps[:, :], mhalf[:, :], ALU.pow).then_inc(S[rstd_name], 1)

            def candidate(b, k):
                if k >= RING:
                    wait(pool, "g_ready", b, k - RING + 1)
                    pool.tensor_tensor(pool_tick[:, k:k + 1], mhalf[:, 0:1], mhalf[:, 0:1], ALU.add)
                pool.tensor_scalar(z_s[:, k % RING, :], a_n[:, :], -1.0 / SHRINKS[k], float(QMAX),
                                   ALU.mult, ALU.add).then_inc(S["z_ready"], 1)

            with pool.Fori(0, B) as b:
                wait(pool, "x_loaded", b, 16)
                wait(pool, "r1_ready", b, 0)
                pool.tensor_tensor(xb[:, :, :], x_nat[:, :, :],
                                   bo_bc[:, :].unsqueeze(1).broadcast_to([P, ST, F]), ALU.add
                                   ).then_inc(S["xb_ready"], 1)
                wait(pool, "a_ready", b, 1)
                pool.tensor_tensor(pool_tick[:, 0:1], mhalf[:, 0:1], mhalf[:, 0:1], ALU.add)
                for k in range(8):
                    candidate(b, k)
                inv_std(b, "mv1", "ve1", "rstd1")
                for k in range(8, NS):
                    candidate(b, k)
                inv_std(b, "mv2", "ve2", "rstd2")
                wait(pool, "qw_ready", b, 1)
                wait(pool, "scale_ready", b, 1)
                wait(pool, "wT_ready", b, 0)
                chunk = w_nat[:, bass.ds(b, 1), :].rearrange("p a n -> p (a n)")
                pool.tensor_tensor(deq[:, :].rearrange("p (n i) -> p n i", i=QBLK),
                                   t_w[:, :].rearrange("p (n i) -> p n i", i=QBLK),
                                   scale[:, :].unsqueeze(2).broadcast_to([P, NB, QBLK]), ALU.mult
                                   ).then_inc(S["deq_ready"], 1)
                pool.wait_ge(once["const_ready"], 2)
                wait(pool, "deq_ready", b, 1)
                pool.tensor_tensor(deq[:, :], deq[:, :], chunk, ALU.subtract).then_inc(S["ddq_ready"], 1)
                pool.wait_ge(once["const_ready"], 2)
                wait(pool, "ddq_ready", b, 1)
                pool.tensor_tensor(wq_nat[:, :], deq[:, :], chunk, ALU.add).then_inc(S["wq_ready"], 1)
            with pool.Fori(0, B) as b:
                inv_std(b, "mv3", "ve3", "rstd3")

        @block.scalar
        def _(act):
            def square(b, k):
                wait(act, "g_ready", b, k + 1)
                if k >= RING:
                    wait(act, "err_ready", b, k - RING + 1)
                act.activation(e_s[:, k % RING, :], g_s[:, k % RING, :], ACT.Square,
                               bias=-QMAX * SHRINKS[k]).then_inc(S["e_ready"], 1)

            for e in range(E):
                act.wait_ge(once["cxT_ready"], e + 1)
                act.copy(cxT[:, e, :, :], two(s_ps[e % 2])).then_inc(once["cxT_sb"], 1)
            act.wait_ge(once["bqh_ready"], 1)
            with act.Fori(0, B) as b:
                wait(act, "ratio_ready", b, 1)
                act.activation(a_n[:, :], t_w[:, :], ACT.Abs).then_inc(S["a_ready"], 1)
                wait(act, "xT_ready", b, 1)
                act.copy(xT[:, :, :], two(tr_ps)).then_inc(S["xT_sb"], 1)
                wait(act, "q_ready", b, 1)
                for k in range(KT):
                    act.activation(qT[:, k, :], two(a_ps)[:, k, :], ACT.Identity, bias=bqh[:, k:k + 1],
                                   scale=0.5).then_inc(S["q_sb"], 1)
                wait(act, "k_ready", b, 1)
                for k in range(KT):
                    act.activation(kTs[:, k, :], two(b_ps)[:, k, :], ACT.Identity, bias=bk_s[:, k:k + 1]
                                   ).then_inc(S["k_sb"], 1)
                wait(act, "v_ready", b, 1)
                act.copy(v_s[:, :, :], two(c_ps)).then_inc(S["v_sb"], 1)

                def probT_copy(h):
                    wait(act, "pt_ready", b, h + 1)
                    act.copy(probT[:, h, :, :], two(pt_ps)).then_inc(S["pt_sb"], 1)

                square(b, 0)
                for h in range(HEADS):
                    wait(act, "nmax_ready", b, h + 1)
                    for s in range(ST):
                        act.activation(prob[:, h, s, :], two(s_ps[h % 2])[:, s, :], ACT.Exp,
                                       bias=nmax[:, h, s:s + 1], accum_out=rsum[:, h, s:s + 1]
                                       ).then_inc(S["p_sb"], 1)
                    square(b, h + 1)
                    if h >= 1:
                        probT_copy(h - 1)
                probT_copy(HEADS - 1)
                square(b, 5)
                square(b, 6)
                wait(act, "fT_ready", b, 1)
                for k in range(KT):
                    act.activation(featT[:, k, :], two(tr_ps)[:, k, :], ACT.Identity, bias=bv_s[:, k:k + 1]
                                   ).then_inc(S["fT_sb"], 1)
                for k in range(7, 12):
                    square(b, k)
                wait(act, "h_ready", b, 1)
                act.activation(tanh_s[:, :, :], two(a_ps), ACT.Tanh, scale=0.5).then_inc(S["tanh_ready"], 1)
                for k in range(12, NS):
                    square(b, k)
                wait(act, "x2T_ready", b, 1)
                act.copy(x2T[:, :, bass.ds(b * T, T)], two(tr_ps)).then_inc(S["x2T_sb"], 1)
                for i, ps in enumerate((w_ps, pt_ps)):
                    wait(act, "wT_ready", b, i + 1)
                    act.copy(wT[:, bass.ds(b, 1), 4 * i:4 * i + 4, :].rearrange("p a j n -> p (a j) n"),
                             ps[:, :].rearrange("p (j n) -> p j n", n=P)).then_inc(S["wT_sb"], 1)
            with act.Fori(0, B) as b:
                for j in range(OT // 2):
                    wait(act, "f1_ready", b, j + 1)
                    if j >= 2:
                        wait(act, "h2_ready", b, j - 1)
                    act.activation(relu_s[:, j % 2, :, :], two(s_ps[j % 2]), ACT.Relu
                                   ).then_inc(S["relu_ready"], 1)

        @block.vector
        def _(dve):
            for k in range(NS):
                dve.memset(shrink[:, k:k + 1], SHRINKS[k]).then_inc(once["shrink_ready"], 1)
            dve.wait_ge(once["shrink_ready"], NS)
            dve.wait_ge(once["b_loaded"], 48)
            dve.tensor_scalar(bqh[:, :], bq_s[:, :], 0.5, None, ALU.mult).then_inc(once["bqh_ready"], 1)

            def blocks(t):
                return t.rearrange("p (n i) -> p n i", i=QBLK)

            def chunk_of(b):
                return w_nat[:, bass.ds(b, 1), :].rearrange("p a n -> p (a n)")

            def normalize_chunk(b):
                dve.tensor_reduce(amax[:, :], blocks(chunk_of(b)), AX.X, ALU.max,
                                  apply_absolute_value=True).then_inc(S["amax_ready"], 1)
                wait(dve, "amax_ready", b, 1)
                dve.tensor_scalar(base[:, :], amax[:, :], 1e-8, 1.0 / QMAX, ALU.max, ALU.mult
                                  ).then_inc(S["base_ready"], 1)
                wait(dve, "base_ready", b, 1)
                dve.reciprocal(rbase[:, :], base[:, :]).then_inc(S["rbase_ready"], 1)
                wait(dve, "rbase_ready", b, 1)
                wait(dve, "wq_ready", b, 0)
                dve.tensor_tensor(blocks(t_w[:, :]), blocks(chunk_of(b)),
                                  rbase[:, :].unsqueeze(2).broadcast_to([P, NB, QBLK]),
                                  ALU.mult).then_inc(S["ratio_ready"], 1)

            def scaled(b, k):
                if k == 0:
                    wait(dve, "a_ready", b, 1)
                wait(dve, "z_ready", b, k + 1)
                if k >= RING:
                    wait(dve, "e_ready", b, k - RING + 1)
                dve.scalar_tensor_tensor(g_s[:, k % RING, :], z_s[:, k % RING, :], SHRINKS[k], a_n[:, :],
                                         ALU.mult, ALU.add).then_inc(S["g_ready"], 1)

            def summed(b, k):
                wait(dve, "e_ready", b, k + 1)
                dve.tensor_reduce(errs[:, k, :], blocks(e_s[:, k % RING, :]), AX.X, ALU.add
                                  ).then_inc(S["err_ready"], 1)

            def candidates(b, k0, k1):
                for k in range(k0, k1):
                    scaled(b, k)
                    if k >= 1:
                        summed(b, k - 1)

            def statistics(b, src, n):
                bst_name, mv_name = f"bst{n}", f"mv{n}"
                for s in range(ST):
                    dve.bn_stats(bst[:, s, :], src[:, s, :]).then_inc(S[bst_name], 1)
                wait(dve, bst_name, b, ST)
                dve.memset(dve_tick[:, n - 1:n], 0.0)
                for s in range(ST):
                    dve.bn_aggr(mv[:, s, :], bst[:, s, :]).then_inc(S[mv_name], 1)

            def normalized(b, dst, src, rstd_name, done):
                wait(dve, rstd_name, b, 1)
                for s in range(ST):
                    dve.tensor_scalar(dst[:, s, :], src[:, s, :], mv[:, s, 0:1], rstd[:, s:s + 1],
                                      ALU.subtract, ALU.mult).then_inc(S[done], 1)

            def masks():
                dve.wait_ge(once["tok_loaded"], 16)
                for i, (dst, op, edge) in enumerate(((mask[:, 0, :], ALU.is_lt, 1), (below[:, 0, :], ALU.is_lt, 2),
                                                     (below[:, 1, :], ALU.is_lt, 3), (mask[:, 3, :], ALU.is_ge, 3))):
                    dve.tensor_scalar(dst, tok_bc[:, :], float(edge * PER_EXPERT), None, op
                                      ).then_inc(once["below_ready"], 1)
                dve.wait_ge(once["below_ready"], 4)
                dve.tensor_tensor(mask[:, 1, :], below[:, 0, :], mask[:, 0, :], ALU.subtract
                                  ).then_inc(once["mask_ready"], 1)
                dve.tensor_tensor(mask[:, 2, :], below[:, 1, :], below[:, 0, :], ALU.subtract
                                  ).then_inc(once["mask_ready"], 1)

            dve.wait_ge(once["w_loaded"], 16 * NCH)
            masks()
            dve.wait_ge(once["mask_ready"], 2)
            dve.wait_ge(once["cxT_ready"], E)
            with dve.Fori(0, B) as b:
                mask_b = mask[:, :, bass.ds(b * T, T)]
                normalize_chunk(b)
                candidates(b, 0, 1)
                for h in range(HEADS):
                    wait(dve, "s_ready", b, h + 1)
                    dve.tensor_reduce(nmax[:, h, :], two(s_ps[h % 2]), AX.X, ALU.max, negate=True
                                      ).then_inc(S["nmax_ready"], 1)
                    candidates(b, h + 1, h + 2)
                wait(dve, "p_sb", b, HEADS * ST)
                dve.reciprocal(rinv[:, :, :], rsum[:, :, :]).then_inc(S["rinv_ready"], 1)
                candidates(b, 5, 6)
                wait(dve, "f_ready", b, 1)
                wait(dve, "rinv_ready", b, 1)
                for s in range(ST):
                    ins = dve.tensor_tensor(
                        feat[:, s, :].rearrange("p (h d) -> p h d", d=DH),
                        two(a_ps)[:, s, :].rearrange("p (h d) -> p h d", d=DH),
                        rinv[:, :, s].unsqueeze(2).broadcast_to([P, HEADS, DH]), ALU.mult)
                ins.then_inc(S["f_sb"], 1)
                candidates(b, 6, 7)
                wait(dve, "o_ready", b, 1)
                wait(dve, "xb_ready", b, 1)
                dve.tensor_tensor(r1[:, :, :], two(b_ps), xb[:, :, :], ALU.add).then_inc(S["r1_ready"], 1)
                wait(dve, "r1_ready", b, 1)
                statistics(b, r1, 1)
                candidates(b, 7, 8)
                normalized(b, x1, r1, "rstd1", "x1_ready")
                candidates(b, 8, 9)
                wait(dve, "x1T_ready", b, 1)
                for e in range(E):
                    dve.tensor_tensor(x1T[:, e, :, :], two(tr_ps),
                                      mask_b[:, e, :].unsqueeze(1).broadcast_to([P, KT, T]), ALU.mult
                                      ).then_inc(S["x1T_sb"], 1)
                candidates(b, 9, 12)
                wait(dve, "tanh_ready", b, 1)
                dve.scalar_tensor_tensor(u_s[:, :, :], tanh_s[:, :, :], 1.0, two(a_ps), ALU.add, ALU.mult
                                         ).then_inc(S["u_ready"], 1)
                wait(dve, "u_ready", b, 1)
                dve.scalar_tensor_tensor(p_s[:, :, :], u_s[:, :, :], 0.5, two(a_ps), ALU.mult, ALU.mult
                                         ).then_inc(S["p_ready"], 1)
                wait(dve, "p_ready", b, 1)
                for e in range(E):
                    dve.tensor_tensor(pm[:, e, :, :], p_s[:, :, :],
                                      mask_b[:, e, :].unsqueeze(1).broadcast_to([P, KT, T]), ALU.mult
                                      ).then_inc(S["pm_ready"], 1)
                candidates(b, 12, NS)
                summed(b, NS - 1)
                wait(dve, "y_ready", b, 1)
                dve.tensor_tensor(r2[:, :, :], two(c_ps), x1[:, :, :], ALU.add).then_inc(S["r2_ready"], 1)
                wait(dve, "r2_ready", b, 1)
                statistics(b, r2, 2)
                wait(dve, "err_ready", b, NS)
                dve.tensor_reduce(emin[:, :], errs[:, :, :].rearrange("p k n -> p n k"), AX.X, ALU.min
                                  ).then_inc(S["emin_ready"], 1)
                wait(dve, "emin_ready", b, 1)
                dve.tensor_tensor(cand[:, :, :], errs[:, :, :],
                                  emin[:, :].unsqueeze(1).broadcast_to([P, NS, NB]), ALU.not_equal
                                  ).then_inc(S["ne_ready"], 1)
                wait(dve, "ne_ready", b, 1)
                dve.scalar_tensor_tensor(cand[:, :, :], cand[:, :, :], FAR,
                                         shrink[:, :].unsqueeze(2).broadcast_to([P, NS, NB]), ALU.mult, ALU.add
                                         ).then_inc(S["cand_ready"], 1)
                wait(dve, "cand_ready", b, 1)
                dve.tensor_reduce(best[:, :], cand[:, :, :].rearrange("p k n -> p n k"), AX.X, ALU.min
                                  ).then_inc(S["best_ready"], 1)
                wait(dve, "best_ready", b, 1)
                wait(dve, "wq_ready", b, 0)
                dve.tensor_tensor(scale[:, :], best[:, :], base[:, :], ALU.mult).then_inc(S["scale_ready"], 1)
                wait(dve, "scale_ready", b, 1)
                dve.reciprocal(rscale[:, :], scale[:, :]).then_inc(S["rscale_ready"], 1)
                wait(dve, "rscale_ready", b, 1)
                wait(dve, "a_ready", b, 1)
                dve.tensor_tensor(blocks(t_w[:, :]), blocks(chunk_of(b)),
                                  rscale[:, :].unsqueeze(2).broadcast_to([P, NB, QBLK]), ALU.mult
                                  ).then_inc(S["tw_ready"], 1)
                wait(dve, "tw_ready", b, 1)
                dve.tensor_scalar(t_w[:, :], t_w[:, :], float(QMAX), -float(QMAX), ALU.min, ALU.max
                                  ).then_inc(S["tc_ready"], 1)
                wait(dve, "tc_ready", b, 1)
                dve.tensor_scalar(t_w[:, :], t_w[:, :], ROUND, -ROUND, ALU.add, ALU.add
                                  ).then_inc(S["qw_ready"], 1)
                wait(dve, "x2_kept", b, 0)
                normalized(b, x2, r2, "rstd2", "x2_ready")
            wait(dve, "x2_kept", B - 1, 16)
            with dve.Fori(0, B) as b:
                for j in range(OT // 2):
                    wait(dve, "relu_ready", b, j + 1)
                    if j == 0:
                        wait(dve, "f2_ready", b, 0)
                    dve.tensor_tensor(h2T[:, 2 * j:2 * j + 2, :], relu_s[:, j % 2, :, :],
                                      relu_s[:, j % 2, :, :], ALU.mult).then_inc(S["h2_ready"], 1)
                wait(dve, "f2_ready", b, 1)
                dve.tensor_tensor(r3[:, :, :], two(c_ps),
                                  x2_all[:, bass.ds(b, 1), :, :].rearrange("p a s f -> p (a s) f"), ALU.add
                                  ).then_inc(S["r3_ready"], 1)
                wait(dve, "r3_ready", b, 1)
                statistics(b, r3, 3)
                wait(dve, "y_kept", b, 0)
                normalized(b, y_out, r3, "rstd3", "y_sb")

        @block.tensor
        def _(pe):
            def turn(ps, src, done):
                for k in range(KT):
                    for s in range(ST):
                        ins = pe.transpose(ps[:, k * T + s * P:k * T + (s + 1) * P],
                                           src[:, s, k * P:(k + 1) * P], ident[:, :])
                ins.then_inc(done, 1)

            def project(ps, wgt, src, done):
                for m in range(KT):
                    for k in range(KT):
                        ins = pe.matmul(two(ps)[:, m, :], wgt[:, k, m * P:(m + 1) * P], src[:, k, :],
                                        start=(k == 0), stop=(k == KT - 1))
                ins.then_inc(done, 1)

            def project_rows(ps, src, wgt, done):
                for s in range(ST):
                    for k in range(KT):
                        ins = pe.matmul(two(ps)[:, s, :], src[:, k, s * P:(s + 1) * P], wgt[:, k, :],
                                        start=(k == 0), stop=(k == KT - 1))
                ins.then_inc(done, 1)

            pe.wait_ge(once["ident_ready"], 1)
            pe.wait_ge(once["cx_loaded"], 16)
            for e in range(E):
                if e >= 2:
                    pe.wait_ge(once["cxT_sb"], e - 1)
                turn(s_ps[e % 2], cx_nat[:, e, :, :], once["cxT_ready"])
            pe.wait_ge(once["cxT_sb"], E)
            pe.wait_ge(once["wqk_loaded"], 32)
            pe.wait_ge(once["wvo_loaded"], 32)
            with pe.Fori(0, B) as b:
                wait(pe, "x_loaded", b, 16)
                wait(pe, "x2T_sb", b, 0)
                turn(tr_ps, x_nat, S["xT_ready"])
                wait(pe, "xT_sb", b, 1)
                wait(pe, "p_ready", b, 0)
                project(a_ps, wq_s, xT, S["q_ready"])
                project(b_ps, wk_s, xT, S["k_ready"])
                wait(pe, "r2_ready", b, 0)
                project_rows(c_ps, xT, wv_s, S["v_ready"])
                wait(pe, "q_sb", b, KT)
                wait(pe, "k_sb", b, KT)

                def scores(h):
                    lo = h % 2 * DH
                    for s in range(ST):
                        ins = pe.matmul(two(s_ps[h % 2])[:, s, :],
                                        qT[lo:lo + DH, h // 2, s * P:(s + 1) * P],
                                        kTs[lo:lo + DH, h // 2, :], start=True, stop=True)
                    ins.then_inc(S["s_ready"], 1)

                def turn_probs(h):
                    wait(pe, "p_sb", b, ST * (h + 1))
                    if h == 0:
                        wait(pe, "wT_sb", b, 0)
                    else:
                        wait(pe, "pt_sb", b, h)
                    turn(pt_ps, prob[:, h, :, :], S["pt_ready"])

                def mix(h):
                    wait(pe, "pt_sb", b, h + 1)
                    for s in range(ST):
                        for k in range(ST):
                            ins = pe.matmul(two(a_ps)[:, s, h * DH:(h + 1) * DH],
                                            probT[:, h, k, s * P:(s + 1) * P],
                                            v_s[:, k, h * DH:(h + 1) * DH], start=(k == 0), stop=(k == ST - 1))
                    return ins

                scores(0)
                scores(1)
                wait(pe, "v_sb", b, 1)
                for h in range(HEADS):
                    turn_probs(h)
                    if h + 2 < HEADS:
                        scores(h + 2)
                    if h >= 1:
                        mix(h - 1)
                mix(HEADS - 1).then_inc(S["f_ready"], 1)
                wait(pe, "f_sb", b, 1)
                turn(tr_ps, feat, S["fT_ready"])
                wait(pe, "fT_sb", b, KT)
                project_rows(b_ps, featT, wo_s, S["o_ready"])
                wait(pe, "x1_ready", b, ST)
                turn(tr_ps, x1, S["x1T_ready"])
                for m in range(KT):
                    for e in range(E):
                        if m == 0:
                            wait(pe, "x1T_sb", b, e + 1)
                        for k in range(KT):
                            ins = pe.matmul(two(a_ps)[:, m, :], cxT[:, e, k, m * P:(m + 1) * P],
                                            x1T[:, e, k, :], start=(e == 0 and k == 0),
                                            stop=(e == E - 1 and k == KT - 1))
                ins.then_inc(S["h_ready"], 1)
                for s in range(ST):
                    for e in range(E):
                        if s == 0:
                            wait(pe, "pm_ready", b, e + 1)
                        for k in range(KT):
                            ins = pe.matmul(two(c_ps)[:, s, :], pm[:, e, k, s * P:(s + 1) * P],
                                            cxT[:, e, k, :], start=(e == 0 and k == 0),
                                            stop=(e == E - 1 and k == KT - 1))
                ins.then_inc(S["y_ready"], 1)
                wait(pe, "x2_ready", b, ST)
                turn(tr_ps, x2, S["x2T_ready"])
                wait(pe, "wq_ready", b, 1)
                for i, ps in enumerate((w_ps, pt_ps)):
                    for j in range(4):
                        at = (4 * i + j) * P
                        ins = pe.transpose(ps[:, j * P:(j + 1) * P], wq_nat[:, at:at + P], ident[:, :])
                    ins.then_inc(S["wT_ready"], 1)
            wait(pe, "x2T_sb", B - 1, 1)
            wait(pe, "wT_sb", B - 1, 2)
            with pe.Fori(0, B) as b:
                for j in range(OT // 2):
                    if j < 2:
                        wait(pe, "relu_ready", b, 0)
                    else:
                        wait(pe, "relu_ready", b, j - 1)
                    for i in range(2):
                        o = 2 * j + i
                        for k in range(KT):
                            ins = pe.matmul(two(s_ps[j % 2])[:, i, :], wT[:, o // 4, o % 4 * KT + k, :],
                                            x2T[:, k, bass.ds(b * T, T)], start=(k == 0), stop=(k == KT - 1))
                    ins.then_inc(S["f1_ready"], 1)
                wait(pe, "r3_ready", b, 0)
                for s in range(ST):
                    for o in range(OT):
                        if s == 0 and o % 2 == 0:
                            wait(pe, "h2_ready", b, o // 2 + 1)
                        ins = pe.matmul(c_ps[:, s * F:(s + 1) * F], h2T[:, o, s * P:(s + 1) * P],
                                        wT[:, NCH // 2:NCH, o, :], start=(o == 0), stop=(o == OT - 1))
                ins.then_inc(S["f2_ready"], 1)


_INS = ["x", "itok_BxS_13_99985", "ctx_2048", "L0_attn_Wq", "L0_attn_bq", "L0_attn_Wk", "L0_attn_bk",
        "L0_attn_Wv", "L0_attn_bv", "L0_attn_Wo", "L0_attn_bo", "L0_ffn_w_fc", "L0_ffn_w_proj"]


def kernel(**inputs):
    import concourse.bacc as bacc
    from concourse.bass_utils import run_bass_kernel_spmd

    nc = bacc.Bacc("TRN2", target_bir_lowering=False, num_devices=1)
    arrays, args = {}, []
    for name in _INS:
        a = np.ascontiguousarray(inputs[name])
        arrays[f"in_{name}_dram"] = a
        args.append(nc.dram_tensor(f"in_{name}_dram", a.shape, mybir.dt.from_np(a.dtype), kind="ExternalInput").ap())
    out = nc.dram_tensor("out_dram", (B, T, F), F32, kind="ExternalOutput").ap()
    build_decoder(nc, *args, out)
    r = run_bass_kernel_spmd(nc, [arrays], core_ids=[0])
    return r.results[0]["out_dram"]
```

```python
from contextlib import ExitStack

import numpy as np
import concourse.bass as bass
from concourse import mybir

F32 = mybir.dt.float32
I32 = mybir.dt.int32
U8 = mybir.dt.uint8
BF16 = mybir.dt.bfloat16
ALU = mybir.AluOpType
ACT = mybir.ActivationFunctionType
AX = mybir.AxisListType

P = 128
B, T, F = 4, 256, 256
HEADS, DH = 4, 64
E = 4
HID = 1024
ST = T // P
KT = F // P
OT = HID // P
VOCAB = 12500
PER_EXPERT = VOCAB // E
EPS = 1e-5
QBLK = 64
QMAX = 15
SHRINKS = [float(np.float32(s)) for s in np.linspace(0.4, 1.0, 16)]
NS = len(SHRINKS)
WCOLS = 2 * HID * F // P
FC_COLS = WCOLS // 2
CH, CH_LAST = 768, 1024
NCH = B + 1
WBLK = WCOLS // P
LAG = 2
RING = 3
ROUND = 1.5 * 2.0 ** 23
CANDS_A1, CANDS_M2, CANDS_M1, CANDS_E2 = 10, 11, 13, 8
FAR = 1000.0

assert B * CH + CH_LAST == WCOLS


def build_decoder(nc, x, tok, ctx_w, Wq, bq, Wk, bk, Wv, bv, Wo, bo, w_fc, w_proj, out):
    with ExitStack() as ctx:
        def sb(name, shape, dt=F32):
            return ctx.enter_context(nc.sbuf_tensor(name, shape, dt))

        def bank(name):
            return ctx.enter_context(nc.psum_tensor(name, [P, 512], F32))

        def sem(name):
            return ctx.enter_context(nc.semaphore(name))

        wq_s, wk_s, wv_s, wo_s = (sb(n, [P, KT, F]) for n in ("wq_s", "wk_s", "wv_s", "wo_s"))
        bq_s, bk_s, bv_s = (sb(n, [P, KT]) for n in ("bq_s", "bk_s", "bv_s"))
        bqh = sb("bqh", [P, KT])
        bo_bc = sb("bo_bc", [P, F])
        cxT = sb("cxT", [P, E, KT, F])
        tok_bc = sb("tok_bc", [P, B * T], I32)
        mask = sb("mask", [P, E, B * T], BF16)
        below = sb("below", [P, 2, B * T], BF16)
        ident = sb("ident", [P, P])
        shrink = sb("shrink", [P, NS])
        mhalf = sb("mhalf", [P, ST])
        eps_s = sb("eps_s", [P, ST])
        w_nat = sb("w_nat", [P, WCOLS])
        wT = sb("wT", [P, WBLK, P])

        wide = sb("wide", [P, B, OT * T])
        prob = wide[:, 0, :].rearrange("p (h s t) -> p h s t", h=HEADS, s=ST)
        probT = wide[:, 1, :].rearrange("p (h s t) -> p h s t", h=HEADS, s=ST)
        x1T = wide[:, 2, :].rearrange("p (e k t) -> p e k t", e=E, k=KT)
        pm = wide[:, 3, :].rearrange("p (e k t) -> p e k t", e=E, k=KT)
        cx_nat = wide[:, 3, :].rearrange("p (e k f) -> p e k f", e=E, k=KT)
        h2T = wide[:, :, :].rearrange("p b (o t) -> p b o t", t=T)

        x_nat = sb("x_nat", [P, ST, F])
        xb = sb("xb", [P, ST, F])
        xT = sb("xT", [P, KT, T])
        qT = sb("qT", [P, KT, T])
        kTs = sb("kTs", [P, KT, T])
        v_s = sb("v_s", [P, ST, F])
        nmax = sb("nmax", [P, HEADS, ST])
        rsum = sb("rsum", [P, HEADS, ST])
        rinv = sb("rinv", [P, HEADS, ST])
        feat = sb("feat", [P, ST, F])
        featT = sb("featT", [P, KT, T])
        r1 = sb("r1", [P, ST, F])
        x1 = sb("x1", [P, ST, F])
        tanh_s = sb("tanh_s", [P, KT, T])
        u_s = sb("u_s", [P, KT, T])
        p_s = sb("p_s", [P, KT, T])
        r2 = sb("r2", [P, ST, F])
        x2 = sb("x2", [P, ST, F])
        x2_all = sb("x2_all", [P, B, ST, F])
        x2T = sb("x2T", [P, KT, B * T])
        bst = sb("bst", [P, 3, ST, 6])
        mv = sb("mv", [P, 3, ST, 2])
        veps = sb("veps", [P, 3, ST])
        rstd = sb("rstd", [P, 3, ST])
        base = sb("base", [P, CH_LAST // QBLK])
        amax = sb("amax", [P, CH_LAST // QBLK])
        rbase = sb("rbase", [P, CH_LAST // QBLK])
        a_n = sb("a_n", [P, CH_LAST])
        z_s = sb("z_s", [P, RING, CH_LAST], U8)
        g_s = sb("g_s", [P, RING, CH_LAST])
        e_s = sb("e_s", [P, RING, CH_LAST])
        errs = sb("errs", [P, NS, CH_LAST // QBLK])
        emin = sb("emin", [P, CH_LAST // QBLK])
        cand = sb("cand", [P, NS, CH_LAST // QBLK])
        best = sb("best", [P, CH_LAST // QBLK])
        scale = sb("scale", [P, CH_LAST // QBLK])
        rscale = sb("rscale", [P, CH_LAST // QBLK])
        t_w = sb("t_w", [P, CH_LAST])
        wq_nat = sb("wq_nat", [P, CH_LAST])
        relu_s = sb("relu_s", [P, 2, 2, T])
        r3 = sb("r3", [P, ST, F])
        y_out = sb("y_out", [P, 2, ST, F])

        tr_ps, pt_ps, s0_ps, s1_ps = (bank(n) for n in ("tr_ps", "pt_ps", "s0_ps", "s1_ps"))
        a_ps, b_ps, h_ps, y_ps = (bank(n) for n in ("a_ps", "b_ps", "h_ps", "y_ps"))
        s_ps = (s0_ps, s1_ps)
        f1_ps = (s0_ps, s1_ps, a_ps, b_ps)
        f2_ps = (h_ps, y_ps)

        def two(ps):
            return ps[:, :].rearrange("p (a t) -> p a t", a=2)

        per = dict(
            x_loaded=16, xT_ready=1, xT_sb=1, xb_ready=1,
            q_ready=1, q_sb=KT, k_ready=1, k_sb=KT, v_ready=1, v_sb=1,
            s_ready=HEADS, nmax_ready=HEADS, p_sb=HEADS * ST, pt_ready=HEADS, pt_sb=HEADS,
            f_ready=1, rinv_ready=1, f_sb=1, fT_ready=1, fT_sb=KT, o_ready=1, r1_ready=1,
            bst1=ST, mv1=ST, ve1=1, rstd1=1, x1_ready=ST, x1T_ready=1, x1T_sb=E,
            h_ready=1, tanh_ready=1, u_ready=1, p_ready=1, pm_ready=E, y_ready=1, r2_ready=1,
            bst2=ST, mv2=ST, ve2=1, rstd2=1, x2_ready=ST, x2T_ready=1, x2T_sb=1, x2_kept=16,
            f1_ready=OT // 2, relu_ready=OT // 2, h2_ready=OT // 2, f2_ready=1, r3_ready=1,
            bst3=ST, mv3=ST, ve3=1, rstd3=1, y_sb=ST, even_y_kept=16, odd_y_kept=16,

            amax_ready=1, base_ready=1, rbase_ready=1, ratio_ready=1, a_ready=1,
            z_ready=NS, g_ready=NS, e_ready=NS, err_ready=NS,
            emin_ready=1, ne_ready=1, cand_ready=1, best_ready=1, scale_ready=1, rscale_ready=1,
            tw_ready=1, tc_ready=1, qw_ready=1, deq_ready=1, ddq_ready=1, wq_ready=1,
            wT_ready=2, wT_sb=2,
        )
        S = {name: sem(name) for name in per}
        once = {name: sem(name) for name in (
            "wqk_loaded", "wvo_loaded", "b_loaded", "bo_loaded", "cx_loaded", "tok_loaded", "fc0_loaded", "fc1_loaded",
            "proj_loaded", "zero_ready", "ident_ready", "const_ready", "shrink_ready", "bqh_ready",
            "below_ready", "mask_ready", "cxT_ready", "cxT_sb")}

        primed = dict(r1_ready=1, x2T_sb=1, x2_kept=1, wT_ready=1, wT_sb=1,
                      wq_ready=1, relu_ready=OT // 2)

        def wait(eng, name, b, n):
            eng.wait_ge(S[name], b * per[name] + n + primed.get(name, 0))

        dve_tick = sb("dve_tick", [P, 3])
        pool_tick = sb("pool_tick", [P, NS])

        y_kept = ("even_y_kept", "odd_y_kept")

        def width(c):
            return CH_LAST if isinstance(c, int) and c == NCH - 1 else CH

        def chunk(t, c):
            return t[:, bass.ds(c * CH, width(c))]

        def blocks(t):
            return t.rearrange("p (n i) -> p n i", i=QBLK)

        def over(t, c):
            n = width(c) // QBLK
            return t[:, 0:n].unsqueeze(2).broadcast_to([P, n, QBLK])

        block = ctx.enter_context(nc.Block())

        @block.sync
        def _(sp):
            def load_x(b):
                sp.dma_start(x_nat[:, :, :].rearrange("p (a s) f -> p a s f", a=1),
                             x[bass.ds(b, 1), :, :].rearrange("a (s p) f -> p a s f", p=P)
                             ).then_inc(S["x_loaded"], 16)

            def reload_x(b):
                wait(sp, "xT_ready", b - 1, 1)
                wait(sp, "xb_ready", b - 1, 1)
                load_x(b)

            def keep_x2(b):
                wait(sp, "x2_ready", b, ST)
                sp.dma_start(x2_all[:, bass.ds(b, 1), :, :],
                             x2[:, :, :].rearrange("p (a s) f -> p a s f", a=1)).then_inc(S["x2_kept"], 16)

            def rows(w):
                return w.rearrange("(k p) n -> p k n", p=P)

            for name, n in primed.items():
                sp.sem_inc(S[name], n)
            load_x(0)
            half = FC_COLS // 2
            for c in range(2):
                sp.dma_start(w_nat[:, c * half:(c + 1) * half].rearrange("p (o i) -> p o i", i=F),
                             w_fc[c * HID // 2:(c + 1) * HID // 2, :].rearrange("(o p) i -> p o i", p=P)
                             ).then_inc(once[f"fc{c}_loaded"], 16)
                if c == 0:
                    sp.dma_start(wq_s[:, :, :], rows(Wq)).then_inc(once["wqk_loaded"], 16)
                    sp.dma_start(wk_s[:, :, :], rows(Wk)).then_inc(once["wqk_loaded"], 16)
                    for s, d in ((bq_s, bq), (bk_s, bk), (bv_s, bv)):
                        sp.dma_start(s[:, :], d.rearrange("(k p) -> p k", p=P), allow_slow_non_contiguous=True
                                     ).then_inc(once["b_loaded"], 16)
                    sp.dma_start(wv_s[:, :, :], rows(Wv)).then_inc(once["wvo_loaded"], 16)
                    sp.dma_start(bo_bc[:, :], bo.rearrange("(a f) -> a f", a=1).broadcast_to([P, F])
                                 ).then_inc(once["bo_loaded"], 16)
                    sp.dma_start(tok_bc[:, :], tok.rearrange("b t -> (b t)").rearrange("(a n) -> a n", a=1)
                                 .broadcast_to([P, B * T])).then_inc(once["tok_loaded"], 16)
                    sp.dma_start(cx_nat, ctx_w.rearrange("e (k p) d -> p e k d", p=P)
                                 ).then_inc(once["cx_loaded"], 16)
                    sp.dma_start(wo_s[:, :, :], rows(Wo)).then_inc(once["wvo_loaded"], 16)
            for d in range(KT):
                sp.dma_start(w_nat[:, FC_COLS + d * HID:FC_COLS + (d + 1) * HID], w_proj[d * P:(d + 1) * P, :]
                             ).then_inc(once["proj_loaded"], 16)
            reload_x(1)
            with sp.Fori(0, B - 2) as b:
                reload_x(b + 2)
                keep_x2(b)
            keep_x2(B - 2)
            keep_x2(B - 1)
            with sp.Fori(0, B // 2) as i:
                for j in range(2):
                    b = i * 2 + j
                    wait(sp, "y_sb", b, ST)
                    sp.dma_start(out[bass.ds(b, 1), :, :].rearrange("a (s p) f -> p a s f", p=P),
                                 y_out[:, j:j + 1, :, :]).then_inc(S[y_kept[j]], 16)
            for j in range(2):
                wait(sp, y_kept[j], B // 2 - 1, 16)

        @block.gpsimd
        def _(pool):
            pool.memset(ident[:, :], 0.0).then_inc(once["zero_ready"], 1)
            pool.memset(mhalf[:, :], -0.5).then_inc(once["const_ready"], 1)
            pool.memset(eps_s[:, :], EPS).then_inc(once["const_ready"], 1)
            pool.wait_ge(once["zero_ready"], 1)
            pool.affine_select(out=ident[:, :], in_=ident[:, :], compare_op=ALU.not_equal, fill=1.0,
                               base=0, pattern=[[-1, P]], channel_multiplier=1).then_inc(once["ident_ready"], 1)
            pool.wait_ge(once["const_ready"], 2)

            def inv_std(b, n):
                i = n - 1
                wait(pool, f"mv{n}", b, ST)
                pool.tensor_tensor(veps[:, i, :], mv[:, i, :, 1], eps_s[:, :], ALU.add).then_inc(S[f"ve{n}"], 1)
                wait(pool, f"ve{n}", b, 1)
                pool.tensor_tensor(rstd[:, i, :], veps[:, i, :], mhalf[:, :], ALU.pow
                                   ).then_inc(S[f"rstd{n}"], 1)

            def with_bias(b):
                wait(pool, "x_loaded", b, 16)
                wait(pool, "r1_ready", b, 0)
                pool.tensor_tensor(xb[:, :, :], x_nat[:, :, :],
                                   bo_bc[:, :].unsqueeze(1).broadcast_to([P, ST, F]), ALU.add
                                   ).then_inc(S["xb_ready"], 1)

            def candidates(c, k0, k1):
                for k in range(k0, k1):
                    if k == 0 or k >= RING:
                        if k == 0:
                            wait(pool, "a_ready", c, 1)
                        else:
                            wait(pool, "g_ready", c, k - RING + 1)
                        pool.tensor_tensor(pool_tick[:, k:k + 1], mhalf[:, 0:1], mhalf[:, 0:1], ALU.add)
                    pool.tensor_scalar(z_s[:, k % RING, 0:width(c)], a_n[:, 0:width(c)], -1.0 / SHRINKS[k],
                                       float(QMAX), ALU.mult, ALU.add).then_inc(S["z_ready"], 1)

            def dequantize(c, step):
                w = width(c)
                if step == 0:
                    wait(pool, "wT_ready", c, 0)
                    wait(pool, "qw_ready", c, 1)
                    pool.tensor_tensor(blocks(t_w[:, 0:w]), blocks(t_w[:, 0:w]), over(scale, c), ALU.mult
                                       ).then_inc(S["deq_ready"], 1)
                elif step == 1:
                    pool.wait_ge(once["const_ready"], 2)
                    wait(pool, "deq_ready", c, 1)
                    pool.tensor_tensor(t_w[:, 0:w], t_w[:, 0:w], chunk(w_nat, c), ALU.subtract
                                       ).then_inc(S["ddq_ready"], 1)
                else:
                    pool.wait_ge(once["const_ready"], 2)
                    wait(pool, "ddq_ready", c, 1)
                    pool.tensor_tensor(wq_nat[:, 0:w], t_w[:, 0:w], chunk(w_nat, c), ALU.add
                                       ).then_inc(S["wq_ready"], 1)

            def candidates_and_dequantize(c):
                candidates(c, 0, 3)
                dequantize(c - 1, 0)
                candidates(c, 3, 5)
                dequantize(c - 1, 1)
                candidates(c, 5, 7)
                dequantize(c - 1, 2)

            pool.wait_ge(once["bo_loaded"], 16)
            with_bias(0)
            candidates(0, 0, CANDS_A1)
            inv_std(0, 1)
            candidates(0, CANDS_A1, NS)
            with pool.Fori(0, B - 1) as b:
                with_bias(b + 1)
                candidates_and_dequantize(b + 1)
                candidates(b + 1, 7, CANDS_M2)
                inv_std(b, 2)
                candidates(b + 1, CANDS_M2, CANDS_M1)
                inv_std(b + 1, 1)
                candidates(b + 1, CANDS_M1, NS)
            candidates_and_dequantize(B)
            inv_std(B - 1, 2)
            candidates(B, 7, NS)
            with pool.Fori(0, B) as b:
                inv_std(b, 3)

        @block.scalar
        def _(act):
            def absolute(c):
                wait(act, "ratio_ready", c, 1)
                act.activation(a_n[:, 0:width(c)], a_n[:, 0:width(c)], ACT.Abs).then_inc(S["a_ready"], 1)

            def squares(c, k0, k1):
                for k in range(k0, k1):
                    wait(act, "g_ready", c, k + 1)
                    if k >= RING:
                        wait(act, "err_ready", c, k - RING + 1)
                    act.activation(e_s[:, k % RING, 0:width(c)], g_s[:, k % RING, 0:width(c)], ACT.Square,
                                   bias=-QMAX * SHRINKS[k]).then_inc(S["e_ready"], 1)

            def copy_xT(b):
                wait(act, "xT_ready", b, 1)
                act.copy(xT[:, :, :], two(tr_ps)).then_inc(S["xT_sb"], 1)

            def copy_qkv(b):
                wait(act, "q_ready", b, 1)
                for k in range(KT):
                    act.activation(qT[:, k, :], two(a_ps)[:, k, :], ACT.Identity, bias=bqh[:, k:k + 1],
                                   scale=0.5).then_inc(S["q_sb"], 1)
                wait(act, "k_ready", b, 1)
                for k in range(KT):
                    act.activation(kTs[:, k, :], two(b_ps)[:, k, :], ACT.Identity, bias=bk_s[:, k:k + 1]
                                   ).then_inc(S["k_sb"], 1)
                wait(act, "v_ready", b, 1)
                act.copy(v_s[:, :, :], two(pt_ps)).then_inc(S["v_sb"], 1)

            def exps(b, h):
                wait(act, "nmax_ready", b, h + 1)
                for s in range(ST):
                    act.activation(prob[:, h, s, :], two(s_ps[h % 2])[:, s, :], ACT.Exp,
                                   bias=nmax[:, h, s:s + 1], accum_out=rsum[:, h, s:s + 1]
                                   ).then_inc(S["p_sb"], 1)

            def copy_probT(b, h):
                wait(act, "pt_ready", b, h + 1)
                act.copy(probT[:, h, :, :], two(pt_ps)).then_inc(S["pt_sb"], 1)

            def copy_featT(b):
                wait(act, "fT_ready", b, 1)
                for k in range(KT):
                    act.activation(featT[:, k, :], two(tr_ps)[:, k, :], ACT.Identity, bias=bv_s[:, k:k + 1]
                                   ).then_inc(S["fT_sb"], 1)

            def tanh(b):
                wait(act, "h_ready", b, 1)
                act.activation(tanh_s[:, :, :], two(h_ps), ACT.Tanh, scale=0.5).then_inc(S["tanh_ready"], 1)

            def copy_x2T(b):
                wait(act, "x2T_ready", b, 1)
                act.copy(x2T[:, :, bass.ds(b * T, T)], two(tr_ps)).then_inc(S["x2T_sb"], 1)

            def copy_wT(c, i):
                n = min(4, width(c) // P - 4 * i)
                at = c * (CH // P) + 4 * i
                wait(act, "wT_ready", c, i + 1)
                act.copy(wT[:, bass.ds(at, n), :], y_ps[:, 0:n * P].rearrange("p (j n) -> p j n", n=P)
                         ).then_inc(S["wT_sb"], 1)

            def copy_cxT(e):
                act.wait_ge(once["cxT_ready"], e + 1)
                act.copy(cxT[:, e, :, :], two(f2_ps[e % 2])).then_inc(once["cxT_sb"], 1)

            copy_xT(0)
            act.wait_ge(once["bqh_ready"], 1)
            copy_qkv(0)
            absolute(0)
            squares(0, 0, 1)
            exps(0, 0)
            exps(0, 1)
            copy_cxT(0)
            copy_cxT(1)
            squares(0, 1, 3)
            copy_probT(0, 0)
            exps(0, 2)
            squares(0, 3, 4)
            copy_probT(0, 1)
            exps(0, 3)
            squares(0, 4, 5)
            copy_cxT(2)
            copy_cxT(3)
            copy_probT(0, 2)
            squares(0, 5, 6)
            copy_probT(0, 3)
            squares(0, 6, 8)
            copy_featT(0)
            squares(0, 8, NS)
            with act.Fori(0, B - 1) as b:
                n = b + 1
                copy_xT(n)
                copy_qkv(n)
                absolute(n)
                squares(n, 0, 2)
                exps(n, 0)
                exps(n, 1)
                copy_probT(n, 0)
                squares(n, 2, 4)
                exps(n, 2)
                tanh(b)
                copy_probT(n, 1)
                squares(n, 4, 5)
                exps(n, 3)
                copy_wT(b, 0)
                squares(n, 5, 6)
                copy_probT(n, 2)
                copy_wT(b, 1)
                squares(n, 6, 7)
                copy_probT(n, 3)
                squares(n, 7, 9)
                copy_featT(n)
                squares(n, 9, 12)
                copy_x2T(b)
                squares(n, 12, NS)
            b = B - 1
            absolute(B)
            squares(B, 0, 1)
            tanh(b)
            copy_wT(b, 0)
            copy_wT(b, 1)
            squares(B, 1, CANDS_E2)
            copy_x2T(b)
            k = CANDS_E2
            for b in range(B):
                for j in range(OT // 2):
                    i = b * OT // 2 + j
                    wait(act, "f1_ready", b, j + 1)
                    act.activation(relu_s[:, i % 2, :, :], two(f1_ps[j]), ACT.Relu).then_inc(S["relu_ready"], 1)
                    if k < NS:
                        squares(B, k, k + 1)
                        k += 1
                    wait(act, "relu_ready", b, j + 1)
                    act.activation(h2T[:, b, 2 * j:2 * j + 2, :], relu_s[:, i % 2, :, :], ACT.Square
                                   ).then_inc(S["h2_ready"], 1)
            copy_wT(B, 0)
            copy_wT(B, 1)

        @block.vector
        def _(dve):
            for k in range(NS):
                dve.memset(shrink[:, k:k + 1], SHRINKS[k]).then_inc(once["shrink_ready"], 1)

            def normalize_chunk(c):
                n, w = width(c) // QBLK, width(c)
                dve.tensor_reduce(amax[:, 0:n], blocks(chunk(w_nat, c)), AX.X, ALU.max,
                                  apply_absolute_value=True).then_inc(S["amax_ready"], 1)
                wait(dve, "amax_ready", c, 1)
                dve.tensor_scalar(base[:, 0:n], amax[:, 0:n], 1e-8, 1.0 / QMAX, ALU.max, ALU.mult
                                  ).then_inc(S["base_ready"], 1)
                wait(dve, "base_ready", c, 1)
                dve.reciprocal(rbase[:, 0:n], base[:, 0:n]).then_inc(S["rbase_ready"], 1)
                wait(dve, "rbase_ready", c, 1)
                dve.tensor_tensor(blocks(a_n[:, 0:w]), blocks(chunk(w_nat, c)), over(rbase, c),
                                  ALU.mult).then_inc(S["ratio_ready"], 1)

            def candidates(c, k0, k1):
                w = width(c)
                for k in range(k0, k1):
                    if k == 0:
                        wait(dve, "a_ready", c, 1)
                    wait(dve, "z_ready", c, k + 1)
                    if k >= RING:
                        wait(dve, "e_ready", c, k - RING + 1)
                    dve.scalar_tensor_tensor(g_s[:, k % RING, 0:w], z_s[:, k % RING, 0:w], SHRINKS[k],
                                             a_n[:, 0:w], ALU.mult, ALU.add).then_inc(S["g_ready"], 1)
                    if k >= LAG:
                        sum_errors(c, k - LAG)

            def sum_errors(c, k):
                n, w = width(c) // QBLK, width(c)
                wait(dve, "e_ready", c, k + 1)
                dve.tensor_reduce(errs[:, k, 0:n], blocks(e_s[:, k % RING, 0:w]), AX.X, ALU.add
                                  ).then_inc(S["err_ready"], 1)

            def choose_scale(c):
                for k in range(NS - LAG, NS):
                    sum_errors(c, k)
                n, w = width(c) // QBLK, width(c)
                wait(dve, "err_ready", c, NS)
                dve.tensor_reduce(emin[:, 0:n], errs[:, :, 0:n].rearrange("p k n -> p n k"), AX.X, ALU.min
                                  ).then_inc(S["emin_ready"], 1)
                wait(dve, "emin_ready", c, 1)
                dve.tensor_tensor(cand[:, :, 0:n], errs[:, :, 0:n],
                                  emin[:, 0:n].unsqueeze(1).broadcast_to([P, NS, n]), ALU.not_equal
                                  ).then_inc(S["ne_ready"], 1)
                wait(dve, "ne_ready", c, 1)
                dve.scalar_tensor_tensor(cand[:, :, 0:n], cand[:, :, 0:n], FAR,
                                         shrink[:, :].unsqueeze(2).broadcast_to([P, NS, n]), ALU.mult, ALU.add
                                         ).then_inc(S["cand_ready"], 1)
                wait(dve, "cand_ready", c, 1)
                dve.tensor_reduce(best[:, 0:n], cand[:, :, 0:n].rearrange("p k n -> p n k"), AX.X, ALU.min
                                  ).then_inc(S["best_ready"], 1)
                wait(dve, "best_ready", c, 1)
                dve.tensor_tensor(scale[:, 0:n], best[:, 0:n], base[:, 0:n], ALU.mult
                                  ).then_inc(S["scale_ready"], 1)
                wait(dve, "scale_ready", c, 1)
                dve.reciprocal(rscale[:, 0:n], scale[:, 0:n]).then_inc(S["rscale_ready"], 1)

            def quantize(c):
                n, w = width(c) // QBLK, width(c)
                wait(dve, "rscale_ready", c, 1)
                wait(dve, "wq_ready", c, 0)
                dve.tensor_tensor(blocks(t_w[:, 0:w]), blocks(chunk(w_nat, c)), over(rscale, c), ALU.mult
                                  ).then_inc(S["tw_ready"], 1)
                wait(dve, "tw_ready", c, 1)
                dve.tensor_scalar(t_w[:, 0:w], t_w[:, 0:w], float(QMAX), -float(QMAX), ALU.min, ALU.max
                                  ).then_inc(S["tc_ready"], 1)
                wait(dve, "tc_ready", c, 1)
                dve.tensor_scalar(t_w[:, 0:w], t_w[:, 0:w], ROUND, -ROUND, ALU.add, ALU.add
                                  ).then_inc(S["qw_ready"], 1)

            def maxima(b, h):
                wait(dve, "s_ready", b, h + 1)
                dve.tensor_reduce(nmax[:, h, :], two(s_ps[h % 2]), AX.X, ALU.max, negate=True
                                  ).then_inc(S["nmax_ready"], 1)

            def inverse_sums(b):
                wait(dve, "p_sb", b, HEADS * ST)
                dve.reciprocal(rinv[:, :, :], rsum[:, :, :]).then_inc(S["rinv_ready"], 1)

            def features(b):
                wait(dve, "f_ready", b, 1)
                wait(dve, "rinv_ready", b, 1)
                for s in range(ST):
                    ins = dve.tensor_tensor(
                        feat[:, s, :].rearrange("p (h d) -> p h d", d=DH),
                        two(a_ps)[:, s, :].rearrange("p (h d) -> p h d", d=DH),
                        rinv[:, :, s].unsqueeze(2).broadcast_to([P, HEADS, DH]), ALU.mult)
                ins.then_inc(S["f_sb"], 1)

            def statistics(b, src, n):
                for s in range(ST):
                    dve.bn_stats(bst[:, n - 1, s, :], src[:, s, :]).then_inc(S[f"bst{n}"], 1)
                wait(dve, f"bst{n}", b, ST)
                dve.memset(dve_tick[:, n - 1:n], 0.0)
                for s in range(ST):
                    dve.bn_aggr(mv[:, n - 1, s, :], bst[:, n - 1, s, :]).then_inc(S[f"mv{n}"], 1)

            def normalized(b, dst, src, n, done):
                wait(dve, f"rstd{n}", b, 1)
                for s in range(ST):
                    dve.tensor_scalar(dst[:, s, :], src[:, s, :], mv[:, n - 1, s, 0:1], rstd[:, n - 1, s:s + 1],
                                      ALU.subtract, ALU.mult).then_inc(S[done], 1)

            def residual1(b):
                wait(dve, "o_ready", b, 1)
                wait(dve, "xb_ready", b, 1)
                dve.tensor_tensor(r1[:, :, :], two(b_ps), xb[:, :, :], ALU.add).then_inc(S["r1_ready"], 1)
                wait(dve, "r1_ready", b, 1)
                statistics(b, r1, 1)

            def masked(dst, src, b, done):
                for e in range(E):
                    dve.tensor_tensor(dst[:, e, :, :], src,
                                      mask[:, e, bass.ds(b * T, T)].unsqueeze(1).broadcast_to([P, KT, T]),
                                      ALU.mult).then_inc(S[done], 1)

            def expert_inputs(b):
                wait(dve, "x1T_ready", b, 1)
                masked(x1T, two(tr_ps), b, "x1T_sb")

            def gate(b):
                wait(dve, "tanh_ready", b, 1)
                dve.scalar_tensor_tensor(u_s[:, :, :], tanh_s[:, :, :], 1.0, two(h_ps), ALU.add, ALU.mult
                                         ).then_inc(S["u_ready"], 1)
                wait(dve, "u_ready", b, 1)
                dve.scalar_tensor_tensor(p_s[:, :, :], u_s[:, :, :], 0.5, two(h_ps), ALU.mult, ALU.mult
                                         ).then_inc(S["p_ready"], 1)
                wait(dve, "p_ready", b, 1)
                masked(pm, p_s[:, :, :], b, "pm_ready")

            def residual2(b):
                wait(dve, "y_ready", b, 1)
                dve.tensor_tensor(r2[:, :, :], two(y_ps), x1[:, :, :], ALU.add).then_inc(S["r2_ready"], 1)
                wait(dve, "r2_ready", b, 1)
                statistics(b, r2, 2)

            def second_norm(b):
                wait(dve, "x2_kept", b, 0)
                normalized(b, x2, r2, 2, "x2_ready")

            def masks():
                dve.wait_ge(once["tok_loaded"], 16)
                for dst, op, edge in ((mask[:, 0, :], ALU.is_lt, 1), (below[:, 0, :], ALU.is_lt, 2),
                                      (below[:, 1, :], ALU.is_lt, 3), (mask[:, 3, :], ALU.is_ge, 3)):
                    dve.tensor_scalar(dst, tok_bc[:, :], float(edge * PER_EXPERT), None, op
                                      ).then_inc(once["below_ready"], 1)
                dve.wait_ge(once["below_ready"], 4)
                dve.tensor_tensor(mask[:, 1, :], below[:, 0, :], mask[:, 0, :], ALU.subtract
                                  ).then_inc(once["mask_ready"], 1)
                dve.tensor_tensor(mask[:, 2, :], below[:, 1, :], below[:, 0, :], ALU.subtract
                                  ).then_inc(once["mask_ready"], 1)

            dve.wait_ge(once["shrink_ready"], NS)
            dve.wait_ge(once["fc0_loaded"], 16)
            normalize_chunk(0)
            dve.wait_ge(once["b_loaded"], 48)
            dve.tensor_scalar(bqh[:, :], bq_s[:, :], 0.5, None, ALU.mult).then_inc(once["bqh_ready"], 1)
            masks()
            dve.wait_ge(once["mask_ready"], 2)
            candidates(0, 0, 1)
            maxima(0, 0)
            maxima(0, 1)
            candidates(0, 1, 3)
            maxima(0, 2)
            candidates(0, 3, 4)
            maxima(0, 3)
            candidates(0, 4, 7)
            inverse_sums(0)
            features(0)
            candidates(0, 7, 9)
            residual1(0)
            candidates(0, 9, 10)
            normalized(0, x1, r1, 1, "x1_ready")
            candidates(0, 10, NS)
            choose_scale(0)
            dve.wait_ge(once["fc1_loaded"], 16)
            dve.wait_ge(once["proj_loaded"], 32)
            with dve.Fori(0, B - 1) as b:
                n = b + 1
                normalize_chunk(n)
                quantize(b)
                candidates(n, 0, 2)
                expert_inputs(b)
                maxima(n, 0)
                maxima(n, 1)
                candidates(n, 2, 4)
                maxima(n, 2)
                candidates(n, 4, 5)
                maxima(n, 3)
                candidates(n, 5, 6)
                gate(b)
                candidates(n, 6, 8)
                inverse_sums(n)
                features(n)
                candidates(n, 8, 10)
                residual2(b)
                candidates(n, 10, 11)
                second_norm(b)
                candidates(n, 11, 12)
                residual1(n)
                candidates(n, 12, 13)
                normalized(n, x1, r1, 1, "x1_ready")
                candidates(n, 13, NS)
                choose_scale(n)
            b = B - 1
            normalize_chunk(B)
            quantize(B - 1)
            expert_inputs(b)
            candidates(B, 0, 2)
            gate(b)
            candidates(B, 2, CANDS_E2 - 1)
            residual2(b)
            candidates(B, CANDS_E2 - 1, CANDS_E2)
            second_norm(b)
            candidates(B, CANDS_E2, NS)
            choose_scale(B)
            quantize(B)
            w = width(B)
            wait(dve, "qw_ready", B, 1)
            dve.tensor_tensor(blocks(t_w[:, 0:w]), blocks(t_w[:, 0:w]), over(scale, B), ALU.mult
                              ).then_inc(S["deq_ready"], 1)
            wait(dve, "deq_ready", B, 1)
            dve.tensor_tensor(t_w[:, 0:w], t_w[:, 0:w], chunk(w_nat, B), ALU.subtract
                              ).then_inc(S["ddq_ready"], 1)
            wait(dve, "ddq_ready", B, 1)
            wait(dve, "wT_ready", B, 0)
            dve.tensor_tensor(wq_nat[:, 0:w], t_w[:, 0:w], chunk(w_nat, B), ALU.add
                              ).then_inc(S["wq_ready"], 1)
            wait(dve, "x2_kept", B - 1, 16)
            for b in range(B):
                wait(dve, "f2_ready", b, 1)
                if b >= 1:
                    wait(dve, "y_sb", b - 1, ST)
                dve.tensor_tensor(r3[:, :, :], two(f2_ps[b % 2]), x2_all[:, b, :, :], ALU.add
                                  ).then_inc(S["r3_ready"], 1)
                wait(dve, "r3_ready", b, 1)
                statistics(b, r3, 3)
                if b >= 2:
                    wait(dve, y_kept[b % 2], b // 2 - 1, 16)
                normalized(b, y_out[:, b % 2, :, :], r3, 3, "y_sb")

        @block.tensor
        def _(pe):
            def turn(ps, src, done):
                for k in range(KT):
                    for s in range(ST):
                        ins = pe.transpose(ps[:, k * T + s * P:k * T + (s + 1) * P],
                                           src[:, s, k * P:(k + 1) * P], ident[:, :])
                ins.then_inc(done, 1)

            def project(ps, wgt, src, done):
                for m in range(KT):
                    for k in range(KT):
                        ins = pe.matmul(two(ps)[:, m, :], wgt[:, k, m * P:(m + 1) * P], src[:, k, :],
                                        start=(k == 0), stop=(k == KT - 1))
                ins.then_inc(done, 1)

            def project_rows(ps, src, wgt, done):
                for s in range(ST):
                    for k in range(KT):
                        ins = pe.matmul(two(ps)[:, s, :], src[:, k, s * P:(s + 1) * P], wgt[:, k, :],
                                        start=(k == 0), stop=(k == KT - 1))
                ins.then_inc(done, 1)

            def turn_x(b):
                wait(pe, "x_loaded", b, 16)
                if not (isinstance(b, int) and b == 0):
                    wait(pe, "x2T_sb", b - 1, 0)
                turn(tr_ps, x_nat, S["xT_ready"])

            def qkv(b):
                wait(pe, "xT_sb", b, 1)
                project(a_ps, wq_s, xT, S["q_ready"])
                project(b_ps, wk_s, xT, S["k_ready"])
                if isinstance(b, int) and b == 0:
                    pe.wait_ge(once["wvo_loaded"], 32)
                project_rows(pt_ps, xT, wv_s, S["v_ready"])

            def scores(b, h):
                if h == 0:
                    wait(pe, "q_sb", b, KT)
                    wait(pe, "k_sb", b, KT)
                lo = h % 2 * DH
                for s in range(ST):
                    ins = pe.matmul(two(s_ps[h % 2])[:, s, :], qT[lo:lo + DH, h // 2, s * P:(s + 1) * P],
                                    kTs[lo:lo + DH, h // 2, :], start=True, stop=True)
                ins.then_inc(S["s_ready"], 1)

            def turn_probs(b, h):
                wait(pe, "p_sb", b, ST * (h + 1))
                if h == 0:
                    wait(pe, "v_sb", b, 1)
                else:
                    wait(pe, "pt_sb", b, h)
                turn(pt_ps, prob[:, h, :, :], S["pt_ready"])

            def mix(b, h):
                wait(pe, "pt_sb", b, h + 1)
                for s in range(ST):
                    for k in range(ST):
                        ins = pe.matmul(two(a_ps)[:, s, h * DH:(h + 1) * DH],
                                        probT[:, h, k, s * P:(s + 1) * P],
                                        v_s[:, k, h * DH:(h + 1) * DH], start=(k == 0), stop=(k == ST - 1))
                if h == HEADS - 1:
                    ins.then_inc(S["f_ready"], 1)

            def turn_feat(b):
                wait(pe, "f_sb", b, 1)
                turn(tr_ps, feat, S["fT_ready"])

            def project_out(b):
                wait(pe, "fT_sb", b, KT)
                project_rows(b_ps, featT, wo_s, S["o_ready"])

            def turn_x1(b):
                wait(pe, "x1_ready", b, ST)
                turn(tr_ps, x1, S["x1T_ready"])

            def experts_in(b, m):
                for e in range(E):
                    if m == 0:
                        wait(pe, "x1T_sb", b, e + 1)
                    for k in range(KT):
                        ins = pe.matmul(two(h_ps)[:, m, :], cxT[:, e, k, m * P:(m + 1) * P],
                                        x1T[:, e, k, :], start=(e == 0 and k == 0),
                                        stop=(e == E - 1 and k == KT - 1))
                if m == KT - 1:
                    ins.then_inc(S["h_ready"], 1)

            def experts_out(b, s):
                for e in range(E):
                    if s == 0:
                        wait(pe, "pm_ready", b, e + 1)
                    for k in range(KT):
                        ins = pe.matmul(two(y_ps)[:, s, :], pm[:, e, k, s * P:(s + 1) * P],
                                        cxT[:, e, k, :], start=(e == 0 and k == 0),
                                        stop=(e == E - 1 and k == KT - 1))
                if s == ST - 1:
                    ins.then_inc(S["y_ready"], 1)

            def turn_x2(b):
                wait(pe, "x2_ready", b, ST)
                turn(tr_ps, x2, S["x2T_ready"])

            def turn_w(c, i):
                n = min(4, width(c) // P - 4 * i)
                if i == 0:
                    wait(pe, "wq_ready", c, 1)
                else:
                    wait(pe, "wT_sb", c, 1)
                for j in range(n):
                    at = (4 * i + j) * P
                    ins = pe.transpose(y_ps[:, j * P:(j + 1) * P], wq_nat[:, at:at + P], ident[:, :])
                ins.then_inc(S["wT_ready"], 1)

            def turn_cx(e):
                if e >= 2:
                    pe.wait_ge(once["cxT_sb"], e - 1)
                turn(f2_ps[e % 2], cx_nat[:, e, :, :], once["cxT_ready"])

            pe.wait_ge(once["ident_ready"], 1)
            turn_x(0)
            pe.wait_ge(once["wqk_loaded"], 32)
            qkv(0)
            scores(0, 0)
            scores(0, 1)
            pe.wait_ge(once["cx_loaded"], 16)
            turn_cx(0)
            turn_cx(1)
            turn_probs(0, 0)
            scores(0, 2)
            mix(0, 0)
            turn_probs(0, 1)
            scores(0, 3)
            mix(0, 1)
            turn_cx(2)
            turn_cx(3)
            turn_probs(0, 2)
            mix(0, 2)
            turn_probs(0, 3)
            mix(0, 3)
            turn_feat(0)
            project_out(0)
            pe.wait_ge(once["cxT_sb"], E)
            with pe.Fori(0, B - 1) as b:
                n = b + 1
                turn_x(n)
                qkv(n)
                turn_x1(b)
                scores(n, 0)
                scores(n, 1)
                experts_in(b, 0)
                turn_probs(n, 0)
                scores(n, 2)
                experts_in(b, 1)
                mix(n, 0)
                turn_probs(n, 1)
                scores(n, 3)
                turn_w(b, 0)
                mix(n, 1)
                turn_probs(n, 2)
                turn_w(b, 1)
                mix(n, 2)
                turn_probs(n, 3)
                wait(pe, "wT_sb", b, 2)
                experts_out(b, 0)
                mix(n, 3)
                experts_out(b, 1)
                turn_feat(n)
                project_out(n)
                turn_x2(b)
            b = B - 1
            wait(pe, "x2T_sb", b, 0)
            turn_x1(b)
            experts_in(b, 0)
            experts_in(b, 1)
            turn_w(b, 0)
            turn_w(b, 1)
            wait(pe, "wT_sb", b, 2)
            experts_out(b, 0)
            experts_out(b, 1)
            turn_x2(b)
            wait(pe, "x2T_sb", b, 1)
            with pe.Fori(0, B) as b:
                for j in range(OT // 2):
                    wait(pe, "relu_ready", b, j + 1 - OT // 2)
                    for i in range(2):
                        o = 2 * j + i
                        for k in range(KT):
                            ins = pe.matmul(two(f1_ps[j])[:, i, :], wT[:, o * KT + k, :],
                                            x2T[:, k, bass.ds(b * T, T)], start=(k == 0), stop=(k == KT - 1))
                    ins.then_inc(S["f1_ready"], 1)
            wait(pe, "r2_ready", B - 1, 1)
            turn_w(B, 0)
            turn_w(B, 1)
            wait(pe, "wT_sb", B, 2)
            proj = wT[:, 2 * OT:WBLK, :].rearrange("p (d o) n -> p d o n", d=KT)
            for b in range(B):
                if b >= 2:
                    wait(pe, "r3_ready", b - 2, 1)
                for s in range(ST):
                    for o in range(OT):
                        if s == 0 and o % 2 == 0:
                            wait(pe, "h2_ready", b, o // 2 + 1)
                        ins = pe.matmul(f2_ps[b % 2][:, s * F:(s + 1) * F], h2T[:, b, o, s * P:(s + 1) * P],
                                        proj[:, :, o, :], start=(o == 0), stop=(o == OT - 1))
                ins.then_inc(S["f2_ready"], 1)


_INS = ["x", "itok_BxS_13_99985", "ctx_2048", "L0_attn_Wq", "L0_attn_bq", "L0_attn_Wk", "L0_attn_bk",
        "L0_attn_Wv", "L0_attn_bv", "L0_attn_Wo", "L0_attn_bo", "L0_ffn_w_fc", "L0_ffn_w_proj"]


def kernel(**inputs):
    import concourse.bacc as bacc
    from concourse.bass_utils import run_bass_kernel_spmd

    nc = bacc.Bacc("TRN2", target_bir_lowering=False, num_devices=1)
    arrays, args = {}, []
    for name in _INS:
        a = np.ascontiguousarray(inputs[name])
        arrays[f"in_{name}_dram"] = a
        args.append(nc.dram_tensor(f"in_{name}_dram", a.shape, mybir.dt.from_np(a.dtype), kind="ExternalInput").ap())
    out = nc.dram_tensor("out_dram", (B, T, F), F32, kind="ExternalOutput").ap()
    build_decoder(nc, *args, out)
    r = run_bass_kernel_spmd(nc, [arrays], core_ids=[0])
    return r.results[0]["out_dram"]
```

```python
from contextlib import ExitStack

import numpy as np
import concourse.bass as bass
from concourse import mybir

F32 = mybir.dt.float32
I32 = mybir.dt.int32
U8 = mybir.dt.uint8
BF16 = mybir.dt.bfloat16
ALU = mybir.AluOpType
ACT = mybir.ActivationFunctionType
AX = mybir.AxisListType

P = 128
B, T, F = 4, 256, 256
HEADS, DH = 4, 64
E = 4
HID = 1024
ST = T // P
KT = F // P
OT = HID // P
VOCAB = 12500
PER_EXPERT = VOCAB // E
EPS = 1e-5
QBLK = 64
QMAX = 15
SHRINKS = [float(np.float32(s)) for s in np.linspace(0.4, 1.0, 16)]
NS = len(SHRINKS)
WCOLS = 2 * HID * F // P
FC_COLS = WCOLS // 2
CH = 640
CH_END = (768, 768)
CH_MAX = max(CH, *CH_END)
NCH = B + 2
STARTS = [c * CH for c in range(B)] + [B * CH, B * CH + CH_END[0]]
WBLK = WCOLS // P
LAG = 2
RING = 4
BY_POOL = (4, 8, 12)
AHEAD = 2
ROUND = 1.5 * 2.0 ** 23
FAR = 1000.0


SOON = min((B - 1) * CH // (2 * F), OT // 2)
HIDDEN = ([(b, j) for b in range(B - 1) for j in range(SOON)]
          + [(b, j) for b in range(B - 1) for j in range(SOON, OT // 2)] + [(B - 1, j) for j in range(OT // 2)])
N_FIRST = 6
N_SOON, N_OTHERS = (B - 1) * SOON, (B - 1) * (OT // 2)
assert N_FIRST <= N_SOON
EARLY_OT = (STARTS[-1] - FC_COLS) // F

assert STARTS[-1] + CH_END[1] == WCOLS and STARTS[-1] == FC_COLS + EARLY_OT * F and B * CH >= FC_COLS


def build_decoder(nc, x, tok, ctx_w, Wq, bq, Wk, bk, Wv, bv, Wo, bo, w_fc, w_proj, out):
    with ExitStack() as ctx:
        def sb(name, shape, dt=F32):
            return ctx.enter_context(nc.sbuf_tensor(name, shape, dt))

        def bank(name):
            return ctx.enter_context(nc.psum_tensor(name, [P, 512], F32))

        def sem(name):
            return ctx.enter_context(nc.semaphore(name))

        wq_s, wk_s, wv_s, wo_s = (sb(n, [P, KT, F]) for n in ("wq_s", "wk_s", "wv_s", "wo_s"))
        bq_s, bk_s, bv_s = (sb(n, [P, KT]) for n in ("bq_s", "bk_s", "bv_s"))
        bqh = sb("bqh", [P, KT])
        bo_bc = sb("bo_bc", [P, F])
        cxT = sb("cxT", [P, E, KT, F])
        tok_bc = sb("tok_bc", [P, B * T], I32)
        mask = sb("mask", [P, E, B * T], BF16)
        ident = sb("ident", [P, P])
        shrink = sb("shrink", [P, NS])
        mhalf = sb("mhalf", [P, ST])
        eps_s = sb("eps_s", [P, ST])
        w_nat = sb("w_nat", [P, WCOLS])
        wT = sb("wT", [P, WBLK, P])

        wide = sb("wide", [P, B, OT * T])
        prob = wide[:, 0, :].rearrange("p (h s t) -> p h s t", h=HEADS, s=ST)
        probT = wide[:, 1, :].rearrange("p (h s t) -> p h s t", h=HEADS, s=ST)
        x1T = wide[:, 2, :].rearrange("p (e k t) -> p e k t", e=E, k=KT)
        pm = wide[:, 3, :].rearrange("p (e k t) -> p e k t", e=E, k=KT)
        cx_nat = wide[:, 3, :].rearrange("p (e k f) -> p e k f", e=E, k=KT)
        h2T = wide[:, :, :].rearrange("p b (o t) -> p b o t", t=T)

        x_all = sb("x_all", [P, B, ST, F])
        xT = sb("xT", [P, KT, B * T])
        qT = sb("qT", [P, KT, T])
        kTs = sb("kTs", [P, KT, T])
        v_s = sb("v_s", [P, B, ST, F])
        nmax = sb("nmax", [P, HEADS, ST])
        rsum = sb("rsum", [P, HEADS, ST])
        rinv = sb("rinv", [P, HEADS, ST])
        feat = sb("feat", [P, ST, F])
        featT = sb("featT", [P, KT, T])
        r1 = sb("r1", [P, ST, F])
        x1 = sb("x1", [P, ST, F])
        gate_s = sb("gate_s", [P, 2, 2, T])
        tanh_s, u_s = gate_s[:, 0, :, :], gate_s[:, 1, :, :]
        p_s = sb("p_s", [P, KT, T])
        r2 = sb("r2", [P, ST, F])
        x2 = sb("x2", [P, ST, F])
        x2T = sb("x2T", [P, KT, B * T])
        bst = sb("bst", [P, 4, ST, 6])
        mv = sb("mv", [P, 4, ST, 2])
        veps = sb("veps", [P, 4, ST])
        rstd = sb("rstd", [P, 4, ST])
        base = sb("base", [P, CH_MAX // QBLK])
        amax = sb("amax", [P, CH_MAX // QBLK])
        rbase = sb("rbase", [P, CH_MAX // QBLK])
        a_n = sb("a_n", [P, CH_MAX])
        z_s = sb("z_s", [P, RING, CH_MAX], U8)
        g_s = sb("g_s", [P, RING, CH_MAX])
        e_s = sb("e_s", [P, RING, CH_MAX])
        errs = sb("errs", [P, NS, CH_MAX // QBLK])
        emin = sb("emin", [P, CH_MAX // QBLK])
        cand = sb("cand", [P, NS, CH_MAX // QBLK])
        best = sb("best", [P, CH_MAX // QBLK])
        scale = sb("scale", [P, CH_MAX // QBLK])
        rscale = sb("rscale", [P, CH_MAX // QBLK])
        t_w = sb("t_w", [P, CH_MAX])
        wq_nat = sb("wq_nat", [P, CH_MAX])
        relu_s = gate_s
        r3 = sb("r3", [P, 2, ST, F])
        y_out = sb("y_out", [P, 2, ST, F])

        tr_ps, pt_ps, s0_ps, s1_ps = (bank(n) for n in ("tr_ps", "pt_ps", "s0_ps", "s1_ps"))
        a_ps, b_ps, h_ps, y_ps = (bank(n) for n in ("a_ps", "b_ps", "h_ps", "y_ps"))
        s_ps = (s0_ps, s1_ps)
        cx_ps = (h_ps, y_ps)
        v_ps = (pt_ps, h_ps, y_ps, h_ps)
        f1_ps = (s0_ps, s1_ps, a_ps, b_ps)
        f2_ps = (h_ps, y_ps, tr_ps, pt_ps)

        def two(ps):
            return ps[:, :].rearrange("p (a t) -> p a t", a=2)

        per = dict(
            xT_ready=1, xT_sb=1, xb_ready=1,
            q_ready=1, q_sb=KT, k_ready=1, k_sb=KT, v_ready=1, v_sb=1,
            s_ready=HEADS, nmax_ready=HEADS, p_sb=HEADS * ST, pt_ready=HEADS, pt_sb=HEADS,
            f_ready=1, rinv_ready=1, f_sb=1, fT_ready=1, fT_sb=KT, o_ready=1, r1_ready=1,
            bst1=ST, mv1=ST, ve1=1, rstd1=1, x1_ready=ST, x1T_ready=1, x1T_sb=E,
            h_ready=1, tanh_ready=1, u_ready=1, p_ready=1, pm_ready=2, pool_pm_ready=E - 2, y_ready=1, r2_ready=1,
            bst2=ST, mv2=ST, ve2=1, rstd2=1, x2_ready=ST, x2T_ready=1, x2T_sb=1, x2_kept=16,
            f1_ready=OT // 2, relu_ready=OT // 2, h2_ready=OT // 2, f2_ready=1, r3_ready=1,
            bst3=ST, mv3=ST, ve3=1, rstd3=1, y_sb=ST, even_y_kept=16, odd_y_kept=16,

            amax_ready=1, base_ready=1, rbase_ready=1, ratio_ready=1, a_ready=1,
            z_ready=NS, g_ready=NS - len(BY_POOL), zs_ready=len(BY_POOL), pool_g_ready=len(BY_POOL),
            e_ready=NS, err_ready=NS,
            emin_ready=1, ne_ready=1, cand_ready=1, best_ready=1, scale_ready=1, rscale_ready=1,
            tw_ready=1, tc_ready=1, qw_ready=1, deq_ready=1, ddq_ready=1, wq_ready=1,
            wT_ready=2, wT_sb=2,
        )
        S = {name: sem(name) for name in per}
        once = {name: sem(name) for name in (
            "x0_loaded", "x_loaded", "wqk_loaded", "wv_loaded", "wo_loaded", "b_loaded", "bo_loaded",
            "cx_loaded", "tok_loaded", "fc0_loaded", "fc1_loaded",
            "proj_loaded", "zero_ready", "ident_ready", "const_ready", "shrink_ready", "bqh_ready",
            "edge_ready", "mask_ready", "cxT_ready", "cxT_sb")}

        primed = dict(x2T_sb=1, x2_kept=1, wT_ready=1, wT_sb=1,
                      wq_ready=1, relu_ready=OT // 2)

        def wait(eng, name, b, n):
            eng.wait_ge(S[name], b * per[name] + n + primed.get(name, 0))

        def before(k):
            return sum(j < k for j in BY_POOL)

        def wait_for_g(eng, c, k):
            if k in BY_POOL:
                wait(eng, "pool_g_ready", c, before(k) + 1)
            else:
                wait(eng, "g_ready", c, k + 1 - before(k))

        dve_tick = sb("dve_tick", [P, 4])
        pool_tick = sb("pool_tick", [P, NS])

        def slot(b, n):
            return n - 1 if n < 3 else 2 + b % 2

        y_kept = ("even_y_kept", "odd_y_kept")

        def width(c):
            return CH_END[c - B] if isinstance(c, int) and c >= B else CH

        def turns(c):
            return -(-width(c) // (4 * P))

        def wait_for_turns(eng, name, c, n):
            if isinstance(c, int) and c == B + 1:
                wait(eng, name, B, turns(B) + n)
            else:
                wait(eng, name, c, n)

        def start(c):
            return STARTS[c] if isinstance(c, int) else c * CH

        def chunk(t, c):
            return t[:, bass.ds(start(c), width(c))]

        def blocks(t):
            return t.rearrange("p (n i) -> p n i", i=QBLK)

        def over(t, c):
            n = width(c) // QBLK
            return t[:, 0:n].unsqueeze(2).broadcast_to([P, n, QBLK])

        block = ctx.enter_context(nc.Block())

        @block.sync
        def _(sp):
            def keep_x2(b):
                wait(sp, "x2_ready", b, ST)
                sp.dma_start(x_all[:, bass.ds(b, 1), :, :],
                             x2[:, :, :].rearrange("p (a s) f -> p a s f", a=1)).then_inc(S["x2_kept"], 16)

            def rows(w):
                return w.rearrange("(k p) n -> p k n", p=P)

            for name, n in primed.items():
                sp.sem_inc(S[name], n)
            sp.dma_start(x_all[:, 0:1, :, :], x[0:1, :, :].rearrange("b (s p) f -> p b s f", p=P)
                         ).then_inc(once["x0_loaded"], 16)
            half = FC_COLS // 2
            for c in range(2):
                sp.dma_start(w_nat[:, c * half:(c + 1) * half].rearrange("p (o i) -> p o i", i=F),
                             w_fc[c * HID // 2:(c + 1) * HID // 2, :].rearrange("(o p) i -> p o i", p=P)
                             ).then_inc(once[f"fc{c}_loaded"], 16)
                if c == 0:
                    sp.dma_start(wq_s[:, :, :], rows(Wq)).then_inc(once["wqk_loaded"], 16)
                    sp.dma_start(wk_s[:, :, :], rows(Wk)).then_inc(once["wqk_loaded"], 16)
                    for s, d in ((bq_s, bq), (bk_s, bk), (bv_s, bv)):
                        sp.dma_start(s[:, :], d.rearrange("(k p) -> p k", p=P), allow_slow_non_contiguous=True
                                     ).then_inc(once["b_loaded"], 16)
                    sp.dma_start(wv_s[:, :, :], rows(Wv)).then_inc(once["wv_loaded"], 16)
                    for b in range(1, B):
                        sp.dma_start(x_all[:, b, :, :], x[b, :, :].rearrange("(s p) f -> p s f", p=P)
                                     ).then_inc(once["x_loaded"], 16)
                    sp.dma_start(bo_bc[:, :], bo.rearrange("(a f) -> a f", a=1).broadcast_to([P, F])
                                 ).then_inc(once["bo_loaded"], 16)
                    sp.dma_start(tok_bc[:, :], tok.rearrange("b t -> (b t)").rearrange("(a n) -> a n", a=1)
                                 .broadcast_to([P, B * T])).then_inc(once["tok_loaded"], 16)
                    sp.dma_start(cx_nat, ctx_w.rearrange("e (k p) d -> p e k d", p=P)
                                 ).then_inc(once["cx_loaded"], 16)
                    sp.dma_start(wo_s[:, :, :], rows(Wo)).then_inc(once["wo_loaded"], 16)
            for d in range(KT):
                sp.dma_start(w_nat[:, FC_COLS:WCOLS].rearrange("p (o d j) -> p o d j", d=KT, j=P)[:, :, d, :],
                             w_proj[d * P:(d + 1) * P, :].rearrange("p (o j) -> p o j", j=P)
                             ).then_inc(once["proj_loaded"], 16)
            with sp.Fori(0, B) as b:
                keep_x2(b)
            with sp.Fori(0, B // 2) as i:
                for j in range(2):
                    b = i * 2 + j
                    wait(sp, "y_sb", b, ST)
                    sp.dma_start(out[bass.ds(b, 1), :, :].rearrange("a (s p) f -> p a s f", p=P),
                                 y_out[:, j:j + 1, :, :]).then_inc(S[y_kept[j]], 16)
            for j in range(2):
                wait(sp, y_kept[j], B // 2 - 1, 16)

        @block.gpsimd
        def _(pool):
            pool.memset(ident[:, :], 0.0).then_inc(once["zero_ready"], 1)
            pool.memset(mhalf[:, :], -0.5).then_inc(once["const_ready"], 1)
            pool.memset(eps_s[:, :], EPS).then_inc(once["const_ready"], 1)
            pool.wait_ge(once["zero_ready"], 1)
            pool.affine_select(out=ident[:, :], in_=ident[:, :], compare_op=ALU.not_equal, fill=1.0,
                               base=0, pattern=[[-1, P]], channel_multiplier=1).then_inc(once["ident_ready"], 1)
            pool.wait_ge(once["const_ready"], 2)

            def inv_std(b, n):
                i = slot(b, n)
                wait(pool, f"mv{n}", b, ST)
                pool.tensor_tensor(veps[:, i, :], mv[:, i, :, 1], eps_s[:, :], ALU.add).then_inc(S[f"ve{n}"], 1)
                wait(pool, f"ve{n}", b, 1)
                pool.tensor_tensor(rstd[:, i, :], veps[:, i, :], mhalf[:, :], ALU.pow
                                   ).then_inc(S[f"rstd{n}"], 1)

            def with_bias(b):
                wait(pool, "xT_ready", b, 1)
                pool.tensor_tensor(x_all[:, b, :, :], x_all[:, b, :, :],
                                   bo_bc[:, :].unsqueeze(1).broadcast_to([P, ST, F]), ALU.add
                                   ).then_inc(S["xb_ready"], 1)

            def candidates(c, k0, k1):
                for k in range(k0, k1):
                    if k == 0 or k >= RING:
                        if k == 0:
                            wait(pool, "a_ready", c, 1)
                        elif k - RING in BY_POOL:
                            wait(pool, "zs_ready", c, before(k - RING) + 1)
                        else:
                            wait_for_g(pool, c, k - RING)
                        pool.tensor_tensor(pool_tick[:, k:k + 1], mhalf[:, 0:1], mhalf[:, 0:1], ALU.add)
                    pool.tensor_scalar(z_s[:, k % RING, 0:width(c)], a_n[:, 0:width(c)], -1.0 / SHRINKS[k],
                                       float(QMAX), ALU.mult, ALU.add).then_inc(S["z_ready"], 1)
                    if k - 1 in BY_POOL:
                        add_a(c, k - 1)

            def add_a(c, k):
                w = width(c)
                wait(pool, "zs_ready", c, before(k) + 1)
                pool.tensor_tensor(g_s[:, k % RING, 0:w], g_s[:, k % RING, 0:w], a_n[:, 0:w], ALU.add
                                   ).then_inc(S["pool_g_ready"], 1)

            def dequantize(c, step):
                w = width(c)
                if step == 0:
                    pool.wait_ge(once["const_ready"], 2)
                    wait(pool, "rscale_ready", c, 1)
                    pool.tensor_tensor(blocks(t_w[:, 0:w]), blocks(chunk(w_nat, c)), over(rscale, c), ALU.mult
                                       ).then_inc(S["tw_ready"], 1)
                elif step == 1:
                    wait(pool, "wT_ready", c, 0)
                    wait(pool, "qw_ready", c, 1)
                    pool.tensor_tensor(blocks(t_w[:, 0:w]), blocks(t_w[:, 0:w]), over(scale, c), ALU.mult
                                       ).then_inc(S["deq_ready"], 1)
                elif step == 2:
                    pool.wait_ge(once["const_ready"], 2)
                    wait(pool, "deq_ready", c, 1)
                    pool.tensor_tensor(t_w[:, 0:w], t_w[:, 0:w], chunk(w_nat, c), ALU.subtract
                                       ).then_inc(S["ddq_ready"], 1)
                else:
                    pool.wait_ge(once["const_ready"], 2)
                    wait(pool, "ddq_ready", c, 1)
                    pool.tensor_tensor(wq_nat[:, 0:w], t_w[:, 0:w], chunk(w_nat, c), ALU.add
                                       ).then_inc(S["wq_ready"], 1)

            def candidates_and_dequantize(c, k0, k1, k2):
                wait(pool, "wq_ready", c - 1, 0)
                candidates(c, 0, k0)
                dequantize(c - 1, 0)
                candidates(c, k0, k1)
                dequantize(c - 1, 1)
                candidates(c, k1, k2)
                dequantize(c - 1, 2)
                candidates(c, k2, 7)
                dequantize(c - 1, 3)

            def masked_p(b):
                for e in range(2, E):
                    pool.wait_ge(once["mask_ready"], 2)
                    wait(pool, "p_ready", b, 1)
                    pool.tensor_tensor(pm[:, e, :, :], p_s[:, :, :],
                                       mask[:, e, bass.ds(b * T, T)].unsqueeze(1).broadcast_to([P, KT, T]),
                                       ALU.mult).then_inc(S["pool_pm_ready"], 1)

            candidates(0, 0, 8)
            pool.wait_ge(once["bo_loaded"], 16)
            with_bias(0)
            candidates(0, 8, 12)
            with_bias(1)
            candidates(0, 12, 14)
            inv_std(0, 1)
            candidates(0, 14, NS)
            for b in range(2, B):
                with_bias(b)
            with pool.Fori(0, B - 1) as b:
                candidates_and_dequantize(b + 1, 1, 4, 5)
                candidates(b + 1, 7, 11)
                masked_p(b)
                candidates(b + 1, 11, 16)
                inv_std(b, 2)
                candidates(b + 1, 16, 16)
                inv_std(b + 1, 1)
                candidates(b + 1, 16, NS)
            candidates_and_dequantize(B, 2, 5, 7)
            masked_p(B - 1)
            candidates(B, 7, 16)
            inv_std(B - 1, 2)
            candidates(B, 16, NS)
            candidates_and_dequantize(B + 1, 1, 6, 6)
            candidates(B + 1, 7, NS)
            for b in range(B):
                inv_std(b, 3)

        @block.scalar
        def _(act):
            def absolute(c):
                wait(act, "ratio_ready", c, 1)
                act.activation(a_n[:, 0:width(c)], a_n[:, 0:width(c)], ACT.Abs).then_inc(S["a_ready"], 1)

            def squares(c, k0, k1):
                w = width(c)
                for k in range(k0, k1):
                    j = k + AHEAD
                    if j in BY_POOL:
                        wait(act, "z_ready", c, j + 1)
                        if j >= RING:
                            wait(act, "e_ready", c, j - RING + 1)
                        act.activation(g_s[:, j % RING, 0:w], z_s[:, j % RING, 0:w], ACT.Identity,
                                       scale=SHRINKS[j], bias=-QMAX * SHRINKS[j]).then_inc(S["zs_ready"], 1)
                    wait_for_g(act, c, k)
                    if k >= RING:
                        wait(act, "err_ready", c, k - RING + 1)
                    act.activation(e_s[:, k % RING, 0:w], g_s[:, k % RING, 0:w], ACT.Square,
                                   bias=0.0 if k in BY_POOL else -QMAX * SHRINKS[k]).then_inc(S["e_ready"], 1)

            def copy_xT(b):
                wait(act, "xT_ready", b, 1)
                act.copy(xT[:, :, b * T:(b + 1) * T], two(tr_ps)).then_inc(S["xT_sb"], 1)

            def copy_qk(b):
                wait(act, "q_ready", b, 1)
                for k in range(KT):
                    act.activation(qT[:, k, :], two(a_ps)[:, k, :], ACT.Identity, bias=bqh[:, k:k + 1],
                                   scale=0.5).then_inc(S["q_sb"], 1)
                wait(act, "k_ready", b, 1)
                for k in range(KT):
                    act.activation(kTs[:, k, :], two(b_ps)[:, k, :], ACT.Identity, bias=bk_s[:, k:k + 1]
                                   ).then_inc(S["k_sb"], 1)

            def copy_v(b):
                wait(act, "v_ready", b, 1)
                act.copy(v_s[:, b, :, :], two(v_ps[b])).then_inc(S["v_sb"], 1)

            def exps(b, h):
                wait(act, "nmax_ready", b, h + 1)
                for s in range(ST):
                    act.activation(prob[:, h, s, :], two(s_ps[h % 2])[:, s, :], ACT.Exp,
                                   bias=nmax[:, h, s:s + 1], accum_out=rsum[:, h, s:s + 1]
                                   ).then_inc(S["p_sb"], 1)

            def copy_probT(b, h):
                wait(act, "pt_ready", b, h + 1)
                act.copy(probT[:, h, :, :], two(pt_ps)).then_inc(S["pt_sb"], 1)

            def copy_featT(b):
                wait(act, "fT_ready", b, 1)
                for k in range(KT):
                    act.activation(featT[:, k, :], two(tr_ps)[:, k, :], ACT.Identity, bias=bv_s[:, k:k + 1]
                                   ).then_inc(S["fT_sb"], 1)

            def tanh(b):
                wait(act, "h_ready", b, 1)
                act.activation(tanh_s, two(h_ps), ACT.Tanh, scale=0.5).then_inc(S["tanh_ready"], 1)

            def copy_x2T(b):
                wait(act, "x2T_ready", b, 1)
                act.copy(x2T[:, :, bass.ds(b * T, T)], two(tr_ps)).then_inc(S["x2T_sb"], 1)

            def copy_wT(c, i, ps):
                n = min(4, width(c) // P - 4 * i)
                at = (STARTS[c] // P if isinstance(c, int) else c * (CH // P)) + 4 * i
                wait_for_turns(act, "wT_ready", c, i + 1)
                act.copy(wT[:, bass.ds(at, n), :], ps[:, 0:n * P].rearrange("p (j n) -> p j n", n=P)
                         ).then_inc(S["wT_sb"], 1)

            def copy_cxT(e):
                act.wait_ge(once["cxT_ready"], e + 1)
                act.copy(cxT[:, e, :, :], two(cx_ps[e % 2])).then_inc(once["cxT_sb"], 1)

            copy_xT(0)
            act.wait_ge(once["bqh_ready"], 1)
            absolute(0)
            squares(0, 0, 1)
            copy_qk(0)
            copy_v(0)
            squares(0, 1, 3)
            exps(0, 0)
            exps(0, 1)
            squares(0, 3, 4)
            copy_probT(0, 0)
            exps(0, 2)
            copy_cxT(0)
            copy_cxT(1)
            squares(0, 4, 5)
            copy_probT(0, 1)
            exps(0, 3)
            copy_cxT(2)
            copy_cxT(3)
            copy_probT(0, 2)
            copy_xT(1)
            squares(0, 5, 6)
            copy_probT(0, 3)
            squares(0, 6, 7)
            copy_v(1)
            squares(0, 7, 9)
            copy_featT(0)
            squares(0, 9, 12)
            for b in range(2, B):
                copy_xT(b)
                copy_v(b)
            squares(0, 12, NS)
            with act.Fori(0, B - 1) as b:
                n = b + 1
                copy_qk(n)
                absolute(n)
                squares(n, 0, 1)
                exps(n, 0)
                exps(n, 1)
                copy_probT(n, 0)
                squares(n, 1, 3)
                exps(n, 2)
                squares(n, 3, 6)
                tanh(b)
                copy_probT(n, 1)
                exps(n, 3)
                copy_wT(b, 0, y_ps)
                copy_probT(n, 2)
                squares(n, 6, 7)
                copy_wT(b, 1, y_ps)
                copy_probT(n, 3)
                squares(n, 7, 11)
                copy_featT(n)
                squares(n, 11, 15)
                copy_x2T(b)
                squares(n, 15, NS)

            def hidden(i0, i1, k0, k1):
                for i in range(i0, i1):
                    b, j = HIDDEN[i]
                    k2, k3 = (k0 + (k1 - k0) * (i + d - i0) // (i1 - i0) for d in range(2))
                    wait(act, "f1_ready", 0, i + 1)
                    act.activation(relu_s[:, i % 2, :, :], two(f1_ps[i % 4]), ACT.Relu).then_inc(S["relu_ready"], 1)
                    squares(B, k2, k3)
                    wait(act, "relu_ready", 0, i + 1)
                    act.activation(h2T[:, b, 2 * j:2 * j + 2, :], relu_s[:, i % 2, :, :], ACT.Square
                                   ).then_inc(S["h2_ready"], 1)

            b = B - 1
            absolute(B)
            squares(B, 0, 2)
            tanh(b)
            squares(B, 2, 3)
            wait(act, "u_ready", b, 1)
            wait(act, "p_ready", b, 1)
            hidden(0, N_FIRST, 3, 10)
            copy_wT(b, 0, tr_ps)
            copy_wT(b, 1, pt_ps)
            hidden(N_FIRST, N_OTHERS, 10, NS)
            copy_x2T(b)
            absolute(B + 1)
            hidden(N_OTHERS, len(HIDDEN), NS, NS)
            squares(B + 1, 0, 6)
            for i in range(turns(B)):
                copy_wT(B, i, f1_ps[i])
            squares(B + 1, 6, NS)
            for i in range(turns(B + 1)):
                copy_wT(B + 1, i, f1_ps[i])

        @block.vector
        def _(dve):
            for k in range(NS):
                dve.memset(shrink[:, k:k + 1], SHRINKS[k]).then_inc(once["shrink_ready"], 1)

            def normalize_chunk(c):
                n, w = width(c) // QBLK, width(c)
                dve.tensor_reduce(amax[:, 0:n], blocks(chunk(w_nat, c)), AX.X, ALU.max,
                                  apply_absolute_value=True).then_inc(S["amax_ready"], 1)
                wait(dve, "amax_ready", c, 1)
                dve.tensor_scalar(base[:, 0:n], amax[:, 0:n], 1e-8, 1.0 / QMAX, ALU.max, ALU.mult
                                  ).then_inc(S["base_ready"], 1)
                wait(dve, "base_ready", c, 1)
                dve.reciprocal(rbase[:, 0:n], base[:, 0:n]).then_inc(S["rbase_ready"], 1)
                wait(dve, "rbase_ready", c, 1)
                dve.tensor_tensor(blocks(a_n[:, 0:w]), blocks(chunk(w_nat, c)), over(rbase, c),
                                  ALU.mult).then_inc(S["ratio_ready"], 1)

            def candidates(c, k0, k1):
                w = width(c)
                for k in range(k0, k1):
                    if k == 0:
                        wait(dve, "a_ready", c, 1)
                    if k not in BY_POOL:
                        wait(dve, "z_ready", c, k + 1)
                        if k >= RING:
                            wait(dve, "e_ready", c, k - RING + 1)
                        dve.scalar_tensor_tensor(g_s[:, k % RING, 0:w], z_s[:, k % RING, 0:w], SHRINKS[k],
                                                 a_n[:, 0:w], ALU.mult, ALU.add).then_inc(S["g_ready"], 1)
                    if k >= LAG:
                        sum_errors(c, k - LAG)

            def sum_errors(c, k):
                n, w = width(c) // QBLK, width(c)
                wait(dve, "e_ready", c, k + 1)
                dve.tensor_reduce(errs[:, k, 0:n], blocks(e_s[:, k % RING, 0:w]), AX.X, ALU.add
                                  ).then_inc(S["err_ready"], 1)

            def choose_scale(c):
                for k in range(NS - LAG, NS):
                    sum_errors(c, k)
                n, w = width(c) // QBLK, width(c)
                wait(dve, "err_ready", c, NS)
                dve.tensor_reduce(emin[:, 0:n], errs[:, :, 0:n].rearrange("p k n -> p n k"), AX.X, ALU.min
                                  ).then_inc(S["emin_ready"], 1)
                wait(dve, "emin_ready", c, 1)
                dve.tensor_tensor(cand[:, :, 0:n], errs[:, :, 0:n],
                                  emin[:, 0:n].unsqueeze(1).broadcast_to([P, NS, n]), ALU.not_equal
                                  ).then_inc(S["ne_ready"], 1)
                wait(dve, "ne_ready", c, 1)
                dve.scalar_tensor_tensor(cand[:, :, 0:n], cand[:, :, 0:n], FAR,
                                         shrink[:, :].unsqueeze(2).broadcast_to([P, NS, n]), ALU.mult, ALU.add
                                         ).then_inc(S["cand_ready"], 1)
                wait(dve, "cand_ready", c, 1)
                dve.tensor_reduce(best[:, 0:n], cand[:, :, 0:n].rearrange("p k n -> p n k"), AX.X, ALU.min
                                  ).then_inc(S["best_ready"], 1)
                wait(dve, "best_ready", c, 1)
                dve.tensor_tensor(scale[:, 0:n], best[:, 0:n], base[:, 0:n], ALU.mult
                                  ).then_inc(S["scale_ready"], 1)
                wait(dve, "scale_ready", c, 1)
                dve.reciprocal(rscale[:, 0:n], scale[:, 0:n]).then_inc(S["rscale_ready"], 1)

            def quantize(c):
                w = width(c)
                wait(dve, "tw_ready", c, 1)
                dve.tensor_scalar(t_w[:, 0:w], t_w[:, 0:w], float(QMAX), -float(QMAX), ALU.min, ALU.max
                                  ).then_inc(S["tc_ready"], 1)
                wait(dve, "tc_ready", c, 1)
                dve.tensor_scalar(t_w[:, 0:w], t_w[:, 0:w], ROUND, -ROUND, ALU.add, ALU.add
                                  ).then_inc(S["qw_ready"], 1)

            def maxima(b, h):
                wait(dve, "s_ready", b, h + 1)
                dve.tensor_reduce(nmax[:, h, :], two(s_ps[h % 2]), AX.X, ALU.max, negate=True
                                  ).then_inc(S["nmax_ready"], 1)

            def inverse_sums(b):
                wait(dve, "p_sb", b, HEADS * ST)
                dve.reciprocal(rinv[:, :, :], rsum[:, :, :]).then_inc(S["rinv_ready"], 1)

            def features(b):
                wait(dve, "f_ready", b, 1)
                wait(dve, "rinv_ready", b, 1)
                for s in range(ST):
                    ins = dve.tensor_tensor(
                        feat[:, s, :].rearrange("p (h d) -> p h d", d=DH),
                        two(a_ps)[:, s, :].rearrange("p (h d) -> p h d", d=DH),
                        rinv[:, :, s].unsqueeze(2).broadcast_to([P, HEADS, DH]), ALU.mult)
                ins.then_inc(S["f_sb"], 1)

            def statistics(b, src, n):
                for s in range(ST):
                    dve.bn_stats(bst[:, slot(b, n), s, :], src[:, s, :]).then_inc(S[f"bst{n}"], 1)
                wait(dve, f"bst{n}", b, ST)
                dve.memset(dve_tick[:, slot(b, n):slot(b, n) + 1], 0.0)
                for s in range(ST):
                    dve.bn_aggr(mv[:, slot(b, n), s, :], bst[:, slot(b, n), s, :]).then_inc(S[f"mv{n}"], 1)

            def normalized(b, dst, src, n, done):
                wait(dve, f"rstd{n}", b, 1)
                i = slot(b, n)
                for s in range(ST):
                    dve.tensor_scalar(dst[:, s, :], src[:, s, :], mv[:, i, s, 0:1], rstd[:, i, s:s + 1],
                                      ALU.subtract, ALU.mult).then_inc(S[done], 1)

            def residual1(b):
                wait(dve, "o_ready", b, 1)
                dve.tensor_tensor(r1[:, :, :].rearrange("p (a s) f -> p a s f", a=1),
                                  two(b_ps).rearrange("p (a s) f -> p a s f", a=1),
                                  x_all[:, bass.ds(b, 1), :, :], ALU.add).then_inc(S["r1_ready"], 1)
                wait(dve, "r1_ready", b, 1)
                statistics(b, r1, 1)

            def masked(dst, src, b, done, experts):
                for e in range(experts):
                    dve.tensor_tensor(dst[:, e, :, :], src,
                                      mask[:, e, bass.ds(b * T, T)].unsqueeze(1).broadcast_to([P, KT, T]),
                                      ALU.mult).then_inc(S[done], 1)

            def expert_inputs(b):
                wait(dve, "x1T_ready", b, 1)
                masked(x1T, two(tr_ps), b, "x1T_sb", E)

            def gate(b):
                wait(dve, "tanh_ready", b, 1)
                dve.scalar_tensor_tensor(u_s, tanh_s, 1.0, two(h_ps), ALU.add, ALU.mult
                                         ).then_inc(S["u_ready"], 1)
                wait(dve, "u_ready", b, 1)
                dve.scalar_tensor_tensor(p_s[:, :, :], u_s, 0.5, two(h_ps), ALU.mult, ALU.mult
                                         ).then_inc(S["p_ready"], 1)
                wait(dve, "p_ready", b, 1)
                masked(pm, p_s[:, :, :], b, "pm_ready", 2)

            def residual2(b):
                wait(dve, "y_ready", b, 1)
                dve.tensor_tensor(r2[:, :, :], two(y_ps), x1[:, :, :], ALU.add).then_inc(S["r2_ready"], 1)
                wait(dve, "r2_ready", b, 1)
                statistics(b, r2, 2)

            def second_norm(b):
                wait(dve, "x2_kept", b, 0)
                normalized(b, x2, r2, 2, "x2_ready")

            def masks():
                dve.wait_ge(once["tok_loaded"], 16)
                for e, op, edge in ((0, ALU.is_lt, 1), (3, ALU.is_ge, 3)):
                    dve.tensor_scalar(mask[:, e, :], tok_bc[:, :], float(edge * PER_EXPERT), None, op
                                      ).then_inc(once["edge_ready"], 1)
                dve.wait_ge(once["edge_ready"], 2)
                for e, op, off in ((1, ALU.is_lt, 0), (2, ALU.is_ge, 3)):
                    dve.scalar_tensor_tensor(mask[:, e, :], tok_bc[:, :], float(2 * PER_EXPERT), mask[:, off, :],
                                             op, ALU.subtract).then_inc(once["mask_ready"], 1)

            dve.wait_ge(once["shrink_ready"], NS)
            dve.wait_ge(once["fc0_loaded"], 16)
            normalize_chunk(0)
            dve.wait_ge(once["b_loaded"], 48)
            dve.tensor_scalar(bqh[:, :], bq_s[:, :], 0.5, None, ALU.mult).then_inc(once["bqh_ready"], 1)
            candidates(0, 0, 3)
            maxima(0, 0)
            maxima(0, 1)
            candidates(0, 3, 5)
            maxima(0, 2)
            candidates(0, 5, 6)
            maxima(0, 3)
            masks()
            candidates(0, 6, 9)
            inverse_sums(0)
            features(0)
            candidates(0, 9, 13)
            wait(dve, "xb_ready", 0, 1)
            residual1(0)
            candidates(0, 13, 14)
            normalized(0, x1, r1, 1, "x1_ready")
            candidates(0, 14, NS)
            choose_scale(0)
            dve.wait_ge(once["mask_ready"], 2)
            dve.wait_ge(once["fc1_loaded"], 16)
            dve.wait_ge(once["proj_loaded"], 32)
            with dve.Fori(0, B - 1) as b:
                n = b + 1
                normalize_chunk(n)
                expert_inputs(b)
                candidates(n, 0, 1)
                maxima(n, 0)
                maxima(n, 1)
                quantize(b)
                candidates(n, 1, 4)
                maxima(n, 2)
                candidates(n, 4, 6)
                maxima(n, 3)
                candidates(n, 6, 7)
                gate(b)
                candidates(n, 7, 9)
                inverse_sums(n)
                features(n)
                candidates(n, 9, 14)
                residual2(b)
                candidates(n, 14, 15)
                second_norm(b)
                wait(dve, "xb_ready", B - 1, 1)
                residual1(n)
                candidates(n, 15, 16)
                normalized(n, x1, r1, 1, "x1_ready")
                candidates(n, 16, NS)
                choose_scale(n)
            b = B - 1
            expert_inputs(b)
            normalize_chunk(B)
            candidates(B, 0, 2)
            quantize(B - 1)
            candidates(B, 2, 3)
            gate(b)
            candidates(B, 3, 11)
            residual2(b)
            candidates(B, 11, 15)
            second_norm(b)
            candidates(B, 15, NS)
            choose_scale(B)
            normalize_chunk(B + 1)
            candidates(B + 1, 0, 3)
            quantize(B)
            candidates(B + 1, 3, NS)
            choose_scale(B + 1)
            c = B + 1
            parts = [(lo, min(lo + 4 * P, width(c))) for lo in range(0, width(c), 4 * P)]

            def part(t, lo, hi):
                return t[:, lo:hi]

            def part_over(t, lo, hi):
                n = (hi - lo) // QBLK
                return t[:, lo // QBLK:hi // QBLK].unsqueeze(2).broadcast_to([P, n, QBLK])

            wait(dve, "rscale_ready", c, 1)
            wait(dve, "wq_ready", c, 0)
            for lo, hi in parts:
                dve.tensor_tensor(blocks(part(t_w, lo, hi)), blocks(part(w_nat, start(c) + lo, start(c) + hi)),
                                  part_over(rscale, lo, hi), ALU.mult).then_inc(S["tw_ready"], 1)
            for i, (lo, hi) in enumerate(parts):
                wait(dve, "tw_ready", c, i + 1)
                dve.tensor_scalar(part(t_w, lo, hi), part(t_w, lo, hi), float(QMAX), -float(QMAX), ALU.min,
                                  ALU.max).then_inc(S["tc_ready"], 1)
            for i, (lo, hi) in enumerate(parts):
                wait(dve, "tc_ready", c, i + 1)
                dve.tensor_scalar(part(t_w, lo, hi), part(t_w, lo, hi), ROUND, -ROUND, ALU.add, ALU.add
                                  ).then_inc(S["qw_ready"], 1)
            for i, (lo, hi) in enumerate(parts):
                wait(dve, "qw_ready", c, i + 1)
                dve.tensor_tensor(blocks(part(t_w, lo, hi)), blocks(part(t_w, lo, hi)), part_over(scale, lo, hi),
                                  ALU.mult).then_inc(S["deq_ready"], 1)
            for i, (lo, hi) in enumerate(parts):
                wait(dve, "deq_ready", c, i + 1)
                dve.tensor_tensor(part(t_w, lo, hi), part(t_w, lo, hi),
                                  part(w_nat, start(c) + lo, start(c) + hi), ALU.subtract
                                  ).then_inc(S["ddq_ready"], 1)
            wait_for_turns(dve, "wT_ready", c, 0)
            for i, (lo, hi) in enumerate(parts):
                wait(dve, "ddq_ready", c, i + 1)
                dve.tensor_tensor(part(wq_nat, lo, hi), part(t_w, lo, hi),
                                  part(w_nat, start(c) + lo, start(c) + hi), ALU.add
                                  ).then_inc(S["wq_ready"], 1)

            def residual3(b):
                wait(dve, "f2_ready", b, 1)
                if b >= 2:
                    wait(dve, "y_sb", b - 2, ST)
                dve.tensor_tensor(r3[:, b % 2, :, :], two(f2_ps[b]), x_all[:, b, :, :], ALU.add
                                  ).then_inc(S["r3_ready"], 1)
                wait(dve, "r3_ready", b, 1)
                statistics(b, r3[:, b % 2, :, :], 3)

            def third_norm(b):
                if b >= 2:
                    wait(dve, y_kept[b % 2], b // 2 - 1, 16)
                normalized(b, y_out[:, b % 2, :, :], r3[:, b % 2, :, :], 3, "y_sb")

            wait(dve, "x2_kept", B - 1, 16)
            residual3(0)
            for b in range(B):
                if b + 1 < B:
                    residual3(b + 1)
                third_norm(b)

        @block.tensor
        def _(pe):
            def turn(ps, src, done):
                for k in range(KT):
                    for s in range(ST):
                        ins = pe.transpose(ps[:, k * T + s * P:k * T + (s + 1) * P],
                                           src[:, s, k * P:(k + 1) * P], ident[:, :])
                ins.then_inc(done, 1)

            def project(ps, wgt, src, done):
                for m in range(KT):
                    for k in range(KT):
                        ins = pe.matmul(two(ps)[:, m, :], wgt[:, k, m * P:(m + 1) * P], src[:, k, :],
                                        start=(k == 0), stop=(k == KT - 1))
                ins.then_inc(done, 1)

            def project_rows(ps, src, wgt, done):
                for s in range(ST):
                    for k in range(KT):
                        ins = pe.matmul(two(ps)[:, s, :], src[:, k, s * P:(s + 1) * P], wgt[:, k, :],
                                        start=(k == 0), stop=(k == KT - 1))
                ins.then_inc(done, 1)

            def turn_x(b):
                if b == 0:
                    pe.wait_ge(once["x0_loaded"], 16)
                else:
                    pe.wait_ge(once["x_loaded"], 16 * (B - 1))
                    wait(pe, "xT_sb", b - 1, 1)
                turn(tr_ps, x_all[:, b, :, :], S["xT_ready"])

            def queries_and_keys(b):
                if not isinstance(b, int):
                    wait(pe, "r1_ready", b - 1, 1)
                xbT = xT[:, :, bass.ds(b * T, T)]
                project(a_ps, wq_s, xbT, S["q_ready"])
                project(b_ps, wk_s, xbT, S["k_ready"])

            def values(b):
                if b in (1, 2):
                    pe.wait_ge(once["cxT_sb"], E)
                elif b == 3:
                    wait(pe, "v_sb", 1, 1)
                wait(pe, "xT_sb", b, 1)
                project_rows(v_ps[b], xT[:, :, b * T:(b + 1) * T], wv_s, S["v_ready"])

            def scores(b, h):
                if h == 0:
                    wait(pe, "q_sb", b, KT)
                    wait(pe, "k_sb", b, KT)
                if h >= 2:
                    wait(pe, "p_sb", b, ST * (h - 1))
                lo = h % 2 * DH
                for s in range(ST):
                    ins = pe.matmul(two(s_ps[h % 2])[:, s, :], qT[lo:lo + DH, h // 2, s * P:(s + 1) * P],
                                    kTs[lo:lo + DH, h // 2, :], start=True, stop=True)
                ins.then_inc(S["s_ready"], 1)

            def turn_probs(b, h):
                wait(pe, "p_sb", b, ST * (h + 1))
                if h > 0:
                    wait(pe, "pt_sb", b, h)
                elif isinstance(b, int):
                    wait(pe, "v_sb", b, 1)
                turn(pt_ps, prob[:, h, :, :], S["pt_ready"])

            def mix(b, h):
                wait(pe, "pt_sb", b, h + 1)
                for s in range(ST):
                    for k in range(ST):
                        ins = pe.matmul(two(a_ps)[:, s, h * DH:(h + 1) * DH],
                                        probT[:, h, k, s * P:(s + 1) * P],
                                        v_s[:, bass.ds(b, 1), k, h * DH:(h + 1) * DH],
                                        start=(k == 0), stop=(k == ST - 1))
                if h == HEADS - 1:
                    ins.then_inc(S["f_ready"], 1)

            def turn_feat(b):
                wait(pe, "f_sb", b, 1)
                turn(tr_ps, feat, S["fT_ready"])

            def project_out(b):
                wait(pe, "fT_sb", b, KT)
                project_rows(b_ps, featT, wo_s, S["o_ready"])

            def turn_x1(b):
                wait(pe, "x1_ready", b, ST)
                turn(tr_ps, x1, S["x1T_ready"])

            def experts_in(b, m):
                for e in range(E):
                    if m == 0:
                        wait(pe, "x1T_sb", b, e + 1)
                    for k in range(KT):
                        ins = pe.matmul(two(h_ps)[:, m, :], cxT[:, e, k, m * P:(m + 1) * P],
                                        x1T[:, e, k, :], start=(e == 0 and k == 0),
                                        stop=(e == E - 1 and k == KT - 1))
                if m == KT - 1:
                    ins.then_inc(S["h_ready"], 1)

            def experts_out(b, s):
                for e in range(E):
                    if s == 0:
                        if e < 2:
                            wait(pe, "pm_ready", b, e + 1)
                        else:
                            wait(pe, "pool_pm_ready", b, e - 1)
                    for k in range(KT):
                        ins = pe.matmul(two(y_ps)[:, s, :], pm[:, e, k, s * P:(s + 1) * P],
                                        cxT[:, e, k, :], start=(e == 0 and k == 0),
                                        stop=(e == E - 1 and k == KT - 1))
                if s == ST - 1:
                    ins.then_inc(S["y_ready"], 1)

            def turn_x2(b):
                wait(pe, "x2_ready", b, ST)
                turn(tr_ps, x2, S["x2T_ready"])

            def turn_w(c, i, ps):
                n = min(4, width(c) // P - 4 * i)
                if i == 0:
                    wait(pe, "wq_ready", c, 1)
                elif ps is y_ps:
                    wait(pe, "wT_sb", c, 1)
                elif isinstance(c, int) and c == B + 1:
                    wait(pe, "wq_ready", c, i + 1)
                for j in range(n):
                    at = (4 * i + j) * P
                    ins = pe.transpose(ps[:, j * P:(j + 1) * P], wq_nat[:, at:at + P], ident[:, :])
                ins.then_inc(S["wT_ready"], 1)

            def turn_cx(e):
                if e >= 2:
                    pe.wait_ge(once["cxT_sb"], e - 1)
                turn(cx_ps[e % 2], cx_nat[:, e, :, :], once["cxT_ready"])

            pe.wait_ge(once["ident_ready"], 1)
            turn_x(0)
            pe.wait_ge(once["wqk_loaded"], 32)
            wait(pe, "xT_sb", 0, 1)
            queries_and_keys(0)
            pe.wait_ge(once["wv_loaded"], 16)
            values(0)
            scores(0, 0)
            scores(0, 1)
            pe.wait_ge(once["cx_loaded"], 16)
            turn_cx(0)
            turn_cx(1)
            turn_probs(0, 0)
            scores(0, 2)
            scores(0, 3)
            mix(0, 0)
            turn_probs(0, 1)
            turn_cx(2)
            turn_cx(3)
            mix(0, 1)
            turn_probs(0, 2)
            turn_x(1)
            mix(0, 2)
            turn_probs(0, 3)
            values(1)
            mix(0, 3)
            turn_feat(0)
            pe.wait_ge(once["wo_loaded"], 16)
            project_out(0)
            for b in range(2, B):
                turn_x(b)
                values(b)
            wait(pe, "v_sb", B - 1, 1)
            with pe.Fori(0, B - 1) as b:
                n = b + 1
                queries_and_keys(n)
                wait(pe, "x2T_sb", b, 0)
                turn_x1(b)
                scores(n, 0)
                scores(n, 1)
                experts_in(b, 0)
                turn_probs(n, 0)
                scores(n, 2)
                scores(n, 3)
                mix(n, 0)
                turn_probs(n, 1)
                experts_in(b, 1)
                turn_w(b, 0, y_ps)
                mix(n, 1)
                turn_probs(n, 2)
                turn_w(b, 1, y_ps)
                mix(n, 2)
                turn_probs(n, 3)
                wait(pe, "wT_sb", b, 2)
                mix(n, 3)
                experts_out(b, 0)
                turn_feat(n)
                experts_out(b, 1)
                project_out(n)
                turn_x2(b)
            def mlp_in(i0, i1):
                for i in range(i0, i1):
                    b, j = HIDDEN[i]
                    wait(pe, "relu_ready", 0, i + 1 - 4)
                    for m in range(2):
                        for k in range(KT):
                            ins = pe.matmul(two(f1_ps[i % 4])[:, m, :], wT[:, (2 * j + m) * KT + k, :],
                                            x2T[:, k, b * T:(b + 1) * T], start=(k == 0), stop=(k == KT - 1))
                    ins.then_inc(S["f1_ready"], 1)

            def mlp_out(b, o0, o1):
                for s in range(ST):
                    for o in range(o0, o1):
                        if (b, s, o) == (0, 0, OT - 1):
                            wait_for_turns(pe, "wT_sb", B + 1, turns(B + 1))
                        if s == 0 and o % 2 == 0:
                            wait(pe, "h2_ready", 0, HIDDEN.index((b, o // 2)) + 1)
                        ins = pe.matmul(f2_ps[b][:, s * F:(s + 1) * F], h2T[:, b, o, s * P:(s + 1) * P],
                                        wT[:, (OT + o) * KT:(OT + o + 1) * KT, :],
                                        start=(o == 0 and s == 0), stop=(o == OT - 1 and s == ST - 1))
                if o1 == OT:
                    ins.then_inc(S["f2_ready"], 1)

            b = B - 1
            wait(pe, "x2T_sb", b - 1, 1)
            turn_x1(b)
            experts_in(b, 0)
            experts_in(b, 1)
            mlp_in(0, N_FIRST)
            turn_w(b, 0, tr_ps)
            turn_w(b, 1, pt_ps)
            experts_out(b, 0)
            experts_out(b, 1)
            mlp_in(N_FIRST, N_SOON)
            wait(pe, "wT_sb", b, 2)
            mlp_in(N_SOON, N_OTHERS)
            turn_x2(b)
            wait(pe, "x2T_sb", b, 1)
            mlp_in(N_OTHERS, len(HIDDEN))
            for i in range(turns(B)):
                wait(pe, "relu_ready", B - 1, i + 1)
                turn_w(B, i, f1_ps[i])
            wait(pe, "wT_sb", B, turns(B))
            wait(pe, "r2_ready", B - 1, 1)
            for b in range(B):
                mlp_out(b, 0, EARLY_OT)
            for i in range(turns(B + 1)):
                turn_w(B + 1, i, f1_ps[i])
            wait_for_turns(pe, "wT_sb", B + 1, 1)
            for b in range(B):
                mlp_out(b, EARLY_OT, OT)


_INS = ["x", "itok_BxS_13_99985", "ctx_2048", "L0_attn_Wq", "L0_attn_bq", "L0_attn_Wk", "L0_attn_bk",
        "L0_attn_Wv", "L0_attn_bv", "L0_attn_Wo", "L0_attn_bo", "L0_ffn_w_fc", "L0_ffn_w_proj"]


def kernel(**inputs):
    import concourse.bacc as bacc
    from concourse.bass_utils import run_bass_kernel_spmd

    nc = bacc.Bacc("TRN2", target_bir_lowering=False, num_devices=1)
    arrays, args = {}, []
    for name in _INS:
        a = np.ascontiguousarray(inputs[name])
        arrays[f"in_{name}_dram"] = a
        args.append(nc.dram_tensor(f"in_{name}_dram", a.shape, mybir.dt.from_np(a.dtype), kind="ExternalInput").ap())
    out = nc.dram_tensor("out_dram", (B, T, F), F32, kind="ExternalOutput").ap()
    build_decoder(nc, *args, out)
    r = run_bass_kernel_spmd(nc, [arrays], core_ids=[0])
    return r.results[0]["out_dram"]
```
